# Optimizing a Trainium2 kernel written in Bass

```python
import numpy as np
import jax
import jax.numpy as jnp

def _softmax(x, axis=-1):
    return jax.nn.softmax(x, axis=axis)

def _gelu(x):
    return jax.nn.gelu(x, approximate=True)

def _silu(x):
    return jax.nn.silu(x)

def _sigmoid(x):
    return jax.nn.sigmoid(x)

def _layernorm(x, axis=-1, eps=1e-05):
    m = jnp.mean(x, axis=axis, keepdims=True)
    v = jnp.var(x, axis=axis, keepdims=True)
    return (x - m) / jnp.sqrt(v + eps)

def _scatter_add(tgt, idx, src, axis=0):
    return tgt.at[idx].add(src)

def _segment_sum(src, seg, n):
    return jax.ops.segment_sum(src, seg, n)
kernel_name = 'mk_vit_tower_d1_tok_img256_r4_9743a2'

def setup_inputs(seed: int=0):
    np.random.seed(seed)
    _w = jnp.asarray

    def _rec_inputs():
        import jax
        import jax.numpy as jnp
        _rk = jax.random.key(seed)
        x = 7.22013e-05 + 1.00017 * jax.random.normal(jax.random.fold_in(_rk, 1), (8, 64, 64, 64), jnp.float32)
        return x
    x = _rec_inputs()

    def _L0_tok_setup():
        import jax, jax.numpy as jnp
        import numpy as np
        K = 3
        PAD = (K - 1) // 2
        BN_EPS = 1e-05

        def _unfold(x):
            b, c, h, w = x.shape
            xp = jnp.pad(x, ((0, 0), (0, 0), (PAD, PAD), (PAD, PAD)))
            shifts = [xp[:, :, i:i + h, j:j + w] for i in range(K) for j in range(K)]
            return jnp.stack(shifts, axis=2)
        key = jax.random.key(seed)
        ks = jax.random.split(key, 4)
        b, c, h, w = (8, 64, 64, 64)
        cr = c // 4
        x = jax.random.normal(ks[0], (b, c, h, w), dtype=jnp.float32)
        conv1_w = jax.random.normal(ks[1], (cr, c), dtype=jnp.float32) * (1.0 / np.sqrt(c))
        conv1_b = jnp.zeros((cr,), dtype=jnp.float32)
        bn_gamma = jnp.ones((cr,), dtype=jnp.float32)
        bn_beta = jnp.zeros((cr,), dtype=jnp.float32)
        bn_mean = jnp.zeros((cr,), dtype=jnp.float32)
        bn_var = jnp.ones((cr,), dtype=jnp.float32)
        conv2_w = jax.random.normal(ks[2], (K * K, cr), dtype=jnp.float32) * (1.0 / np.sqrt(cr))
        conv2_b = jnp.zeros((K * K,), dtype=jnp.float32)
        return {'x': x, 'conv1_w': conv1_w, 'conv1_b': conv1_b, 'bn_gamma': bn_gamma, 'bn_beta': bn_beta, 'bn_mean': bn_mean, 'bn_var': bn_var, 'conv2_w': conv2_w, 'conv2_b': conv2_b}
    _L0_tok_all = _L0_tok_setup()
    _L0_tok_in = {k: v for k, v in _L0_tok_all.items() if k in ('conv1_w', 'conv1_b', 'bn_gamma', 'bn_beta', 'bn_mean', 'bn_var', 'conv2_w', 'conv2_b')}
    del _L0_tok_all

    def _L0_attn_setup():
        import jax, jax.numpy as jnp
        import numpy as np
        B, N, C = (8, 2048, 64)
        HEADS, DH, KR = (8, 32, 4)
        INNER = HEADS * DH
        FF = 4 * C
        EPS = 1e-05

        def layernorm(x, g, b):
            mu = jnp.mean(x, axis=-1, keepdims=True)
            var = jnp.mean((x - mu) ** 2, axis=-1, keepdims=True)
            return (x - mu) * jax.lax.rsqrt(var + EPS) * g + b
        key = jax.random.key(seed)
        ks = jax.random.split(key, 16)
        s = 0.02
        return {'x': jax.random.normal(ks[0], (B, N, C), jnp.float32), 'ln1_g': jnp.ones((C,), jnp.float32), 'ln1_b': jnp.zeros((C,), jnp.float32), 'Wx': jax.random.normal(ks[1], (C, INNER), jnp.float32) * s, 'bx': jnp.zeros((INNER,), jnp.float32), 'Wq': jax.random.normal(ks[2], (DH, KR), jnp.float32) * s, 'Wk': jax.random.normal(ks[3], (DH, KR), jnp.float32) * s, 'Wv': jax.random.normal(ks[4], (DH, DH), jnp.float32) * s, 'Wo': jax.random.normal(ks[5], (INNER, C), jnp.float32) * s, 'bo': jnp.zeros((C,), jnp.float32), 'ln2_g': jnp.ones((C,), jnp.float32), 'ln2_b': jnp.zeros((C,), jnp.float32), 'W1': jax.random.normal(ks[6], (C, FF), jnp.float32) * s, 'b1': jnp.zeros((FF,), jnp.float32), 'W2': jax.random.normal(ks[7], (FF, C), jnp.float32) * s, 'b2': jnp.zeros((C,), jnp.float32)}
    _L0_attn_all = _L0_attn_setup()
    _L0_attn_in = {k: v for k, v in _L0_attn_all.items() if k in ('ln1_g', 'ln1_b', 'Wx', 'bx', 'Wq', 'Wk', 'Wv', 'Wo', 'bo', 'ln2_g', 'ln2_b', 'W1', 'b1', 'W2', 'b2')}
    del _L0_attn_all

    def _L0_ffn_setup():
        import jax, jax.numpy as jnp
        import numpy as np
        B, T, IN_DIM = (64, 64, 64)
        HID, OUT_DIM = (128, 64)
        N_LAYERS, N_EXPERTS, N_SHARED = (2, 16, 1)
        key = jax.random.key(seed)
        ks = jax.random.split(key, 10)
        s = 0.02
        x = jax.random.normal(ks[0], (B, T, IN_DIM), dtype=jnp.float32)
        route_id = jax.random.randint(ks[1], (B,), 0, N_EXPERTS)
        Wi = jax.random.normal(ks[2], (HID, IN_DIM), dtype=jnp.float32) * s
        bi = jnp.zeros((HID,), dtype=jnp.float32)
        Wr = jax.random.normal(ks[3], (N_LAYERS, N_EXPERTS, HID, HID), dtype=jnp.float32) * s
        br = jax.random.normal(ks[4], (N_LAYERS, N_EXPERTS, HID), dtype=jnp.float32) * s
        Ws = jax.random.normal(ks[5], (N_LAYERS, N_SHARED, HID, HID), dtype=jnp.float32) * s
        bs = jax.random.normal(ks[6], (N_LAYERS, N_SHARED, HID), dtype=jnp.float32) * s
        Wo = jax.random.normal(ks[7], (OUT_DIM, HID), dtype=jnp.float32) * s
        bo = jnp.zeros((OUT_DIM,), dtype=jnp.float32)
        return {'x': x, 'route_id': route_id, 'Wi': Wi, 'bi': bi, 'Wr': Wr, 'br': br, 'Ws': Ws, 'bs': bs, 'Wo': Wo, 'bo': bo}
    _L0_ffn_all = _L0_ffn_setup()
    _L0_ffn_in = {k: v for k, v in _L0_ffn_all.items() if k in ('route_id', 'Wi', 'bi', 'Wr', 'br', 'Ws', 'bs', 'Wo', 'bo')}
    del _L0_ffn_all
    return {'x': x, 'L0_tok_conv1_w': _L0_tok_in['conv1_w'], 'L0_tok_conv1_b': _L0_tok_in['conv1_b'], 'L0_tok_bn_gamma': _L0_tok_in['bn_gamma'], 'L0_tok_bn_beta': _L0_tok_in['bn_beta'], 'L0_tok_bn_mean': _L0_tok_in['bn_mean'], 'L0_tok_bn_var': _L0_tok_in['bn_var'], 'L0_tok_conv2_w': _L0_tok_in['conv2_w'], 'L0_tok_conv2_b': _L0_tok_in['conv2_b'], 'L0_attn_ln1_g': _L0_attn_in['ln1_g'], 'L0_attn_ln1_b': _L0_attn_in['ln1_b'], 'L0_attn_Wx': _L0_attn_in['Wx'], 'L0_attn_bx': _L0_attn_in['bx'], 'L0_attn_Wq': _L0_attn_in['Wq'], 'L0_attn_Wk': _L0_attn_in['Wk'], 'L0_attn_Wv': _L0_attn_in['Wv'], 'L0_attn_Wo': _L0_attn_in['Wo'], 'L0_attn_bo': _L0_attn_in['bo'], 'L0_attn_ln2_g': _L0_attn_in['ln2_g'], 'L0_attn_ln2_b': _L0_attn_in['ln2_b'], 'L0_attn_W1': _L0_attn_in['W1'], 'L0_attn_b1': _L0_attn_in['b1'], 'L0_attn_W2': _L0_attn_in['W2'], 'L0_attn_b2': _L0_attn_in['b2'], 'L0_ffn_route_id': _L0_ffn_in['route_id'], 'L0_ffn_Wi': _L0_ffn_in['Wi'], 'L0_ffn_bi': _L0_ffn_in['bi'], 'L0_ffn_Wr': _L0_ffn_in['Wr'], 'L0_ffn_br': _L0_ffn_in['br'], 'L0_ffn_Ws': _L0_ffn_in['Ws'], 'L0_ffn_bs': _L0_ffn_in['bs'], 'L0_ffn_Wo': _L0_ffn_in['Wo'], 'L0_ffn_bo': _L0_ffn_in['bo']}

def reference(x, L0_tok_conv1_w, L0_tok_conv1_b, L0_tok_bn_gamma, L0_tok_bn_beta, L0_tok_bn_mean, L0_tok_bn_var, L0_tok_conv2_w, L0_tok_conv2_b, L0_attn_ln1_g, L0_attn_ln1_b, L0_attn_Wx, L0_attn_bx, L0_attn_Wq, L0_attn_Wk, L0_attn_Wv, L0_attn_Wo, L0_attn_bo, L0_attn_ln2_g, L0_attn_ln2_b, L0_attn_W1, L0_attn_b1, L0_attn_W2, L0_attn_b2, L0_ffn_route_id, L0_ffn_Wi, L0_ffn_bi, L0_ffn_Wr, L0_ffn_br, L0_ffn_Ws, L0_ffn_bs, L0_ffn_Wo, L0_ffn_bo):
    import jax
    import jax.numpy as jnp

    def _L0_tok_ref(x, conv1_w, conv1_b, bn_gamma, bn_beta, bn_mean, bn_var, conv2_w, conv2_b):
        import jax, jax.numpy as jnp
        import numpy as np
        K = 3
        PAD = (K - 1) // 2
        BN_EPS = 1e-05

        def _unfold(x):
            b, c, h, w = x.shape
            xp = jnp.pad(x, ((0, 0), (0, 0), (PAD, PAD), (PAD, PAD)))
            shifts = [xp[:, :, i:i + h, j:j + w] for i in range(K) for j in range(K)]
            return jnp.stack(shifts, axis=2)
        b, c, h, w = x.shape
        y = jnp.einsum('oc,bchw->bohw', conv1_w, x) + conv1_b[None, :, None, None]
        y = (y - bn_mean[None, :, None, None]) * (bn_gamma[None, :, None, None] * jax.lax.rsqrt(bn_var + BN_EPS)[None, :, None, None]) + bn_beta[None, :, None, None]
        y = jax.nn.relu(y)
        wdyn = jnp.einsum('ok,bkhw->bohw', conv2_w, y) + conv2_b[None, :, None, None]
        patches = _unfold(x)
        out = jnp.einsum('bckhw,bkhw->bchw', patches, wdyn)
        return out.reshape(b, h * w, c)

    def _L0_attn_ref(x, ln1_g, ln1_b, Wx, bx, Wq, Wk, Wv, Wo, bo, ln2_g, ln2_b, W1, b1, W2, b2):
        import jax, jax.numpy as jnp
        import numpy as np
        B, N, C = (8, 2048, 64)
        HEADS, DH, KR = (8, 32, 4)
        INNER = HEADS * DH
        FF = 4 * C
        EPS = 1e-05

        def layernorm(x, g, b):
            mu = jnp.mean(x, axis=-1, keepdims=True)
            var = jnp.mean((x - mu) ** 2, axis=-1, keepdims=True)
            return (x - mu) * jax.lax.rsqrt(var + EPS) * g + b
        b, n, c = x.shape
        h = layernorm(x, ln1_g, ln1_b)
        xm = h @ Wx + bx
        xm = xm.reshape(b, n, HEADS, DH).transpose(0, 2, 1, 3)
        q = jax.nn.softmax(xm @ Wq, axis=-1)
        k = jax.nn.softmax(xm @ Wk, axis=-2)
        v = xm @ Wv
        kv = jnp.einsum('bhnr,bhnd->bhrd', k, v)
        qkv = jnp.einsum('bhnr,bhrd->bhnd', q, kv)
        attn = qkv.transpose(0, 2, 1, 3).reshape(b, n, INNER) @ Wo + bo
        fx = attn + x
        h2 = layernorm(fx, ln2_g, ln2_b)
        m = jax.nn.gelu(h2 @ W1 + b1, approximate=False) @ W2 + b2
        return m + fx

    def _L0_ffn_ref(x, route_id, Wi, bi, Wr, br, Ws, bs, Wo, bo):
        import jax, jax.numpy as jnp
        import numpy as np
        B, T, IN_DIM = (64, 64, 64)
        HID, OUT_DIM = (128, 64)
        N_LAYERS, N_EXPERTS, N_SHARED = (2, 16, 1)
        flat = x.reshape(-1, x.shape[-1])
        n_tok = flat.shape[0]
        route = jnp.repeat(route_id, n_tok // route_id.shape[0])
        h = jax.nn.relu(flat @ Wi.T + bi)
        n_layers, n_experts = (Wr.shape[0], Wr.shape[1])
        for l in range(n_layers):
            shared = (jnp.einsum('nd,shd->snh', h, Ws[l]) + bs[l][:, None, :]).mean(axis=0)
            routed = jnp.zeros_like(h)
            for e in range(n_experts):
                ye = h @ Wr[l, e].T + br[l, e]
                routed = routed + jnp.where((route == e)[:, None], ye, 0.0)
            h = jax.nn.relu(shared + routed + h)
        out = h @ Wo.T + bo
        return out.reshape(*x.shape[:-1], out.shape[-1])
    h = _L0_tok_ref(x, L0_tok_conv1_w, L0_tok_conv1_b, L0_tok_bn_gamma, L0_tok_bn_beta, L0_tok_bn_mean, L0_tok_bn_var, L0_tok_conv2_w, L0_tok_conv2_b)
    h = h + _L0_attn_ref(_layernorm(h, axis=-1), L0_attn_ln1_g, L0_attn_ln1_b, L0_attn_Wx, L0_attn_bx, L0_attn_Wq, L0_attn_Wk, L0_attn_Wv, L0_attn_Wo, L0_attn_bo, L0_attn_ln2_g, L0_attn_ln2_b, L0_attn_W1, L0_attn_b1, L0_attn_W2, L0_attn_b2)
    h = h + _L0_ffn_ref(_layernorm(h, axis=-1), L0_ffn_route_id, L0_ffn_Wi, L0_ffn_bi, L0_ffn_Wr, L0_ffn_br, L0_ffn_Ws, L0_ffn_bs, L0_ffn_Wo, L0_ffn_bo)
    return h

_drawn_inputs = setup_inputs


def setup_inputs(seed=0):
    import zlib

    import numpy as np

    out = dict(_drawn_inputs(seed))
    spreads = {'L0_tok_conv1_b': (0.0, 0.1),
     'L0_tok_bn_gamma': (1.0, 0.2),
     'L0_tok_bn_beta': (0.0, 0.1),
     'L0_tok_bn_mean': (0.0, 0.1),
     'L0_tok_bn_var': (1.0, 0.2),
     'L0_tok_conv2_b': (0.0, 0.1),
     'L0_attn_ln1_g': (1.0, 0.6),
     'L0_attn_ln1_b': (0.0, 0.8),
     'L0_attn_bx': (0.0, 0.8),
     'L0_attn_bo': (0.0, 0.573),
     'L0_attn_ln2_g': (1.0, 0.6),
     'L0_attn_ln2_b': (0.0, 0.8),
     'L0_attn_b1': (0.0, 0.8),
     'L0_attn_b2': (0.0, 0.531),
     'L0_ffn_bi': (0.0, 0.8),
     'L0_ffn_bo': (0.0, 0.692)}
    factors = {'L0_attn_Wx': 8.0,
     'L0_attn_Wq': 8.0,
     'L0_attn_Wk': 8.0,
     'L0_attn_Wv': 8.0,
     'L0_attn_Wo': 8.0,
     'L0_attn_W1': 6.375,
     'L0_attn_W2': 5.69,
     'L0_ffn_Wi': 8.0,
     'L0_ffn_Wr': 8.0,
     'L0_ffn_br': 8.0,
     'L0_ffn_Ws': 8.0,
     'L0_ffn_bs': 8.0,
     'L0_ffn_Wo': 4.483}
    for name, (base, spread) in spreads.items():
        noise = np.random.default_rng([zlib.crc32(name.encode()), seed]).standard_normal(out[name].shape)
        drawn = base * np.exp(spread * noise) if base else spread * noise
        out[name] = jnp.asarray(drawn.astype(out[name].dtype))
    for name, factor in factors.items():
        out[name] = (out[name] * factor).astype(out[name].dtype)
    return out
```

```python
from contextlib import ExitStack
from collections import namedtuple

import numpy as np
import concourse.bass as bass
from concourse import mybir

F32, F16, BF16, I32 = mybir.dt.float32, mybir.dt.float16, mybir.dt.bfloat16, mybir.dt.int32
ALU = mybir.AluOpType
ACT = mybir.ActivationFunctionType
AX = mybir.AxisListType

P = 128
IMAGES, CH, ROWS, W = 8, 64, 64, 64
HR = ROWS // 2
COLS = HR * W
CHUNKS = 4
CW = COLS // CHUNKS
TPC = HR // CHUNKS
CR, TAPS = 16, 9
PR, PW = 4, 16
PK = (PR + 2) * (PW + 2)
RG, WP = HR // PR, W // PW
HEADS, DH, KR = 8, 32, 4
HKR = HEADS * KR
FF = 4 * W
HID = 128
EXPERTS, LAYERS = 16, 2
SEGS = 8
SEGC = CH // SEGS
EPS = 1e-5
EW = LAYERS * HID + LAYERS
WE_RING = 4

Y_HI_ROWS, Y_LO_ROW, Y_ONE_ROW, Y_ROWS = 96, 64, 96, 99
B_CONV, B_QK, B_ATT, B_MLP, B_FFN, B_ALL = 0, 96, 160, 224, 288, 352

WEIGHT_LOADS, PREP_DVE, PREP_MM = 94, 4, 4
LN_STEPS = {0: 17, 2: 12, 3: 12}
Q_STEPS, K_STEPS = 5, 5

Image = namedtuple("Image", "i h p")


def after(eng, sem, value):
    if not isinstance(value, int) or value > 0:
        eng.wait_ge(sem, value)


class Banks:

    def __init__(self, banks, uses, filled, freed):
        self.place = {}
        count = {b: 0 for b in banks}
        for n, use in enumerate(uses):
            b = banks[n % len(banks)]
            self.place[use] = (b, count[b])
            count[b] += 1
        self.count, self.filled, self.freed = count, filled, freed

    def claim(self, pe, im, *use, needs=()):
        b, k = self.place[use]
        least = {b: k}
        for n in needs:
            c, m = self.place[n]
            least[c] = max(least.get(c, 0), m + 1)
        for c, m in least.items():
            after(pe, self.freed[c], im.i * self.count[c] + m)
        return b

    def full(self, eng, im, *use):
        b, k = self.place[use]
        after(eng, self.filled[b], im.i * self.count[b] + (k + 1))
        return b

    def taken(self, eng, im, *use):
        b, k = self.place[use]
        after(eng, self.freed[b], im.i * self.count[b] + (k + 1))


def slot_order():
    o = [("load", "A"), ("qt", "B", 0), ("qt", "B", 1)]
    o += [("attend", "B", c) for c in range(CHUNKS)]
    o += [("norm2", "B")]
    o += [("conv", "A", c) for c in range(CHUNKS)]
    for c in range(CHUNKS):
        o += [("regroup", "A", c), ("filters", "A", 0, c), ("filters", "A", 1, c)]
    o += [("patches", "A", 0), ("patches", "A", 1)]
    for c in range(CHUNKS):
        if c + 1 < CHUNKS:
            o += [("patches", "A", 2 * c + 2), ("patches", "A", 2 * c + 3)]
        if 2 * c + 5 < RG:
            o += [("regroup", "A", 2 * c + 4), ("regroup", "A", 2 * c + 5)]
        o += [("involve", "A", c)]
    o += [("split2", "B", 0), ("split2", "B", 1), ("norm0", "A")]
    o += [("z3t", "C", c) for c in range(CHUNKS)]
    o += [("ffn", "C", t) for t in range(5)]
    o += [("ft", "B", 0), ("ft", "B", 1)]
    o += [("scale", "A", 0), ("scale", "A", 1)]
    o += [("w1", "B", 0, k) for k in range(4)]
    for c in range(CHUNKS):
        for k in range(4):
            if c + 1 < CHUNKS:
                o.append(("w1", "B", c + 1, k))
            o.append(("w2", "B", c, k))
        if c + 2 < CHUNKS:
            o.append(("ft", "B", c + 2))
    o += [("norm3", "B")]
    o += [("zt", "A", 0)]
    for c in range(CHUNKS):
        if c + 1 < CHUNKS:
            o += [("zt", "A", c + 1)]
        o += [("logits", "A", c)]
    o += [("kmax", "A"), ("ffn", "C", 5), ("ffn", "C", 6), ("kshift", "A"), ("ffn", "C", 7)]
    o += [("ffn", "C", 8), ("ffn", "C", 9), ("pool", "A")]
    o += [("out", "C", c) for c in range(CHUNKS)]
    o += [("mix", "A"), ("mixt", "A"), ("split3", "B", 0), ("split3", "B", 1)]
    return o


def tower_kernel(nc, A, out):
    ctx = ExitStack()
    with ctx:
        def sb(name, shape, dt=F32):
            return ctx.enter_context(nc.sbuf_tensor(name, shape, dt))

        def sem(name):
            return ctx.enter_context(nc.semaphore(name))

        ident = sb("ident", [P, P])
        ident16 = sb("ident16", [P, P], F16)
        bandmask = sb("bandmask", [PK, W])
        headcols = sb("headcols", [P, 2, P])
        headrows = sb("headrows", [P, 4])
        ypick = sb("ypick", [Y_ROWS, 2, 3])
        ones_col = sb("ones_col", [P, 1])
        ones3 = sb("ones3", [3, CW], BF16)
        neg_half = sb("neg_half", [P, HR])
        factor = sb("factor", [P, 4, HR])
        HALF, QUARTER, PER_W, EPSILON = range(4)

        conv_w = sb("conv_w", [P, Y_HI_ROWS])
        tap_w = sb("tap_w", [Y_ROWS, 2, PR, 3, PR + 2, PW + 2], F16)
        qk_w = sb("qk_w", [P, 2 * 2 * HKR])
        head_w = sb("head_w", [P, HEADS, W])
        head_b = sb("head_b", [P, W])
        w1_hh = sb("w1_hh", [P, FF], F16)
        w1_l0 = sb("w1_l0", [P, FF], F16)
        b1_col = sb("b1_col", [P, 2])
        w2_hi = sb("w2_hi", [P, 2, W], F16)
        w2_lo = sb("w2_lo", [P, 2, W], F16)
        wi_hh = sb("wi_hh", [P, HID], F16)
        wi_l0 = sb("wi_l0", [P, HID], F16)
        bi_col = sb("bi_col", [P, 1])
        fo_w = sb("fo_w", [P, W])
        bias_rows = sb("bias_rows", [3, B_ALL], BF16)

        xpad = sb("xpad", [P, HR + 2, W + 2])
        y16 = sb("y16", [Y_ROWS, COLS], F16)
        xrun = sb("xrun", [P, 4, WP, PR + 2, PW + 2])
        xpatch = sb("xpatch", [PK, 4, WP, P])
        wide = sb("wide", [P, 2, COLS])
        h0 = [sb(f"h0_{p}", [P, COLS]) for p in range(2)]
        zn = sb("zn", [P, COLS])
        z = sb("z", [P, COLS])
        zT = sb("zT", [P, 2, CW])
        lg = sb("lg", [P, HR, 2 * HKR])
        q = sb("q", [P, HR, HKR])
        qT = sb("qT", [P, 2 * CHUNKS, P])
        sp2 = sb("sp2", [P, HR, 2 * W], F16)
        sp3 = sb("sp3", [P, HR, 2 * W], F16)
        fT = sb("fT", [P, 2, TPC * P], F16)
        gelu = sb("gelu", [P, 2, 2, 512])
        ge_hi = sb("ge_hi", [P, 3, 2, 512], F16)
        ge_lo = sb("ge_lo", [P, 3, 2, 512], F16)
        h1 = [sb(f"h1_{p}", [P, COLS]) for p in range(2)]
        n3 = sb("n3", [P, COLS])
        z3T = sb("z3T", [P, HR, 2, CH], F16)
        hid_a = sb("hid_a", [P, 2, 512])
        hid_b = sb("hid_b", [P, 2, 512])
        ew = sb("ew", [P, WE_RING, EW])
        route = sb("route", [1, IMAGES * SEGS], I32)
        filt = [wide[0:PK, hh, :] for hh in range(2)]
        hid_c = wide[:, :, :].rearrange("p a n -> p (a n)").rearrange("p (t hh c) -> p t hh c", hh=2, c=CH)

        bn = {k: sb(f"bn{k}", [P, HR, 6]) for k in (0, 2, 3)}
        st = {k: sb(f"st{k}", [P, 8, HR]) for k in (0, 2, 3)}
        kmx = sb("kmx", [P, HKR])
        kmb = sb("kmb", [HKR, P])
        kmc = sb("kmc", [HKR, 1])
        ksum = sb("ksum", [P, 4, HKR])
        qmx = sb("qmx", [P, HR, HEADS])
        qden = sb("qden", [P, HR, HEADS])
        qinv = sb("qinv", [P, HR, HEADS])
        khT = sb("khT", [P, HKR])
        kinv = sb("kinv", [P, 1])
        gT4 = sb("gT4", [P, 4, HKR])
        gmix = sb("gmix", [P, 4, W])
        psum = ctx.enter_context(nc.psum_tensor("psum", [P, 8, 512], F32))

        s_wx = h1[1][0:W, 0:256]
        s_wxT = h1[1][:, 256:512].rearrange("p (b d w) -> p b d w", b=2, d=2)
        s_bdqk = h1[1][:, 512:544]
        s_bdv = h1[1][:, 576:704]
        s_wo = h1[1][:, 704:832].rearrange("p (b c) -> p b c", b=2)
        s_wom = h1[1][:, 832:1344].rearrange("p (b h c) -> p b h c", b=2, h=4)
        s_w2 = zn[:, 0:P].rearrange("p (f c) -> p f c", f=2)
        s_w1 = h1[1][:, 1344:1600]
        s_w1g = h1[1][:, 1600:1856]
        s_vxT = h1[1][:, 1856:1984].rearrange("p (b w) -> p b w", b=2)
        s_wi = n3[:, 0:128].rearrange("p (d w) -> p d w", d=2)
        s_fo = n3[0:W, 128:256]
        s_cw = n3[0:Y_HI_ROWS, 256:384]
        s_cp = n3[0:Y_HI_ROWS, 384:392]
        s_cb3 = n3[0:Y_HI_ROWS, 392:395]
        s_cols = n3[:, 400:416]
        s_u3 = n3[:, 416:422].rearrange("p (b k) -> p b k", b=2)
        s_vbx = n3[:, 448:704].rearrange("p (b k) -> p b k", b=2)
        s_w2f = n3[0:Y_ROWS, 704:713]
        s_w2h = n3[0:Y_ROWS, 720:729]
        s_w2r = n3[0:Y_ROWS, 736:745]
        s_w2a = n3[0:Y_ROWS, 752:770].rearrange("p (h k) -> p h k", h=2)
        s_wiT = n3[:, 784:912]
        s_brf = n3[0:3, 912:912 + B_ALL]
        s_brr = n3[0:3, 1280:1280 + B_ALL]
        s_bra = n3[0:3, 1664:1664 + B_ALL]
        w2h16, w2m16, w2l16 = [zn[0:Y_ROWS, 128 + 8 * k:136 + 8 * k].bitcast(F16)[:, 0:TAPS] for k in range(3)]
        w2d16 = zn[0:Y_ROWS, 160:178].bitcast(F16).rearrange("p (h i j) -> p h i j", h=2, i=3)
        brh, brm, brl = [zn[0:3, 192 + 176 * k:368 + 176 * k].bitcast(BF16) for k in range(3)]
        e_nat = [v[:, :].rearrange("p (e k) -> p e k", e=EXPERTS) for v in h1]
        e_turn = [v[:, :, :].rearrange("p t w -> p (t w)").bitcast(F32).rearrange("p (e k) -> p e k", e=EXPERTS)
                  for v in (sp2, sp3)]
        e_ws = gelu[:, 0, 0, 0:LAYERS * HID].rearrange("p (l k) -> p l k", l=LAYERS)
        e_b = gelu[0:LAYERS * EXPERTS, 0, 1, 0:2 * HID].rearrange("p (a k) -> p a k", a=2)
        e_bT = sb("e_bT", [P, EXPERTS, LAYERS])
        expert_w = nc.dram_tensor("expert_w", [EXPERTS, P, EW], F32, kind="Internal").ap()

        zeroed = sem("zeroed")
        weights_in = sem("weights_in")
        prep_mm, prep_dve = sem("prep_mm"), sem("prep_dve")
        prep_link, var_eps, pow_done = sem("prep_link"), sem("var_eps"), sem("pow_done")
        experts_in, experts_sum, experts_out = sem("experts_in"), sem("experts_sum"), sem("experts_out")
        turned, turned_in = sem("turned"), sem("turned_in")
        filled = [sem(f"filled{b}") for b in range(8)]
        freed = [sem(f"freed{b}") for b in range(8)]
        x_in, regrouped = sem("x_in"), sem("regrouped")
        y_hi = sem("y_hi")
        bn_done = {k: sem(f"bn_done{k}") for k in (0, 2, 3)}
        ln_step = {k: sem(f"ln_step{k}") for k in (0, 2, 3)}
        z_ready, zn_ready = sem("z_ready"), sem("zn_ready")
        q_step, k_step, q_exp, k_exp = sem("q_step"), sem("k_step"), sem("q_exp"), sem("k_exp")
        s1_ready, n2_ready, hi2, lo2 = sem("s1_ready"), sem("n2_ready"), sem("hi2"), sem("lo2")
        ge_high, ge_low = sem("ge_high"), sem("ge_low")
        n3_ready, hi3, lo3 = sem("n3_ready"), sem("hi3"), sem("lo3")
        ew_in = [sem(f"ew_in{k}") for k in range(WE_RING)]
        h1_dma = [sem(f"h1_dma{p}") for p in range(2)]

        uses = {"A": [], "B": [], "M": [], "C": []}
        for name, stage, *args in slot_order():
            if name == "ffn":
                t, = args
                uses["C"] += [("wi", t)] * (t < SEGS) + [("e1", t - 1)] * (1 <= t <= SEGS) + [("e2", t - 2)] * (t >= 2)
            elif name == "w2":
                uses["M"] += [("w2", args[0])] * (args[1] == 0)
            elif name in ("conv", "filters", "patches", "involve", "zt", "logits", "kmax", "kshift", "pool", "mix",
                          "mixt", "qt", "attend", "ft", "w1", "z3t", "out"):
                uses[stage].append((name, *args))
        bank_a = Banks([0, 1, 2], uses["A"], filled, freed)
        bank_b = Banks([3, 4], uses["B"], filled, freed)
        bank_m = Banks([5], uses["M"], filled, freed)
        bank_c = Banks([6, 7], uses["C"], filled, freed)

        def before(im):
            return Image(im.i - 1, None, None)

        def run(steps, images):
            for name, stage, *args in slot_order():
                if name in steps and stage in images:
                    steps[name](images[stage], *args)

        def slots(eng, steps, experts=None):
            def images(s):
                at = {"A": s, "B": s - 1, "C": s - 2}
                return {k: Image(i, i // 2, i % 2) for k, i in at.items() if 0 <= i < IMAGES}

            run(steps, images(0))
            if experts:
                experts()
            run(steps, images(1))
            with eng.Fori(0, IMAGES // 2 - 1) as j:
                for d in range(2):
                    run(steps, {"A": Image(2 * j + (2 + d), j + 1, d), "B": Image(2 * j + (1 + d), j + d, 1 - d),
                                "C": Image(2 * j + d, j, d)})
            run(steps, images(IMAGES))
            run(steps, images(IMAGES + 1))

        def tiles(ap):
            return ap.rearrange("p (t w) -> p t w", w=W)

        def chunk(ap, c):
            return ap[:, CW * c:CW * c + CW]

        block = ctx.enter_context(nc.Block())

        @block.sync
        def _(sp):
            n_in = [0]

            def load(dst, src, slow=False):
                n_in[0] += 1
                sp.dma_start(dst, src, allow_slow_non_contiguous=slow).then_inc(weights_in, 16)

            def col(v, a, n):
                return v[a:a + n].unsqueeze(1)

            def load_x(im):
                x = A["x"][im.i]
                sp.dma_start(xpad[0:CH, 1:HR + 2, 1:W + 1], x[:, 0:HR + 1, :]).then_inc(x_in, 16)
                sp.dma_start(xpad[CH:P, 0:HR + 1, 1:W + 1], x[:, HR - 1:ROWS, :]).then_inc(x_in, 16)

            sp.wait_ge(zeroed, 1)
            load_x(Image(0, 0, 0))
            for dst, name in ((ident, "k_ident"), (ident16, "k_ident16"), (bandmask, "k_bandmask"),
                              (headcols, "k_headcols"), (headrows, "k_headrows"), (ypick, "k_ypick")):
                load(dst[tuple(slice(None) for _ in dst.shape)], A[name])
            for g, half in enumerate((0, 0, 1, 1, 0, 1)):
                load(s_cw[CR * g:CR * g + CR, CH * half:CH * half + CH], A["L0_tok_conv1_w"])
                for k, name in enumerate(("conv1_b", "bn_gamma", "bn_beta", "bn_mean", "bn_var")):
                    load(s_cp[CR * g:CR * g + CR, k:k + 1], col(A["L0_tok_" + name], 0, CR))
                load(s_w2f[CR * g:CR * g + CR, :], A["L0_tok_conv2_w"].rearrange("k o -> o k"), slow=True)
            for r in range(3):
                load(s_w2f[Y_ONE_ROW + r:Y_ONE_ROW + r + 1, :], A["L0_tok_conv2_b"].unsqueeze(0))
                for a, name in ((B_ATT, "L0_attn_bo"), (B_MLP, "L0_attn_b2"), (B_FFN, "L0_ffn_bo")):
                    load(s_brf[r:r + 1, a:a + W], A[name].unsqueeze(0))
            load(s_wx, A["L0_attn_Wx"])
            for h in range(4):
                load(s_bdqk[DH * h:DH * h + DH, KR * h:KR * h + KR], A["L0_attn_Wq"])
                load(s_bdqk[DH * h:DH * h + DH, 16 + KR * h:16 + KR * h + KR], A["L0_attn_Wk"])
                load(s_bdv[DH * h:DH * h + DH, DH * h:DH * h + DH], A["L0_attn_Wv"])
            load(s_wo, A["L0_attn_Wo"].rearrange("(b p) c -> p b c", p=P))
            for d in range(2):
                load(s_w1[W * d:W * d + W, :], A["L0_attn_W1"])
                load(s_wi[:, d, :], A["L0_ffn_Wi"])
                load(s_cols[W * d:W * d + W, 0:1], col(A["L0_attn_ln1_g"], 0, W))
                load(s_cols[W * d:W * d + W, 4:5], col(A["L0_attn_ln2_g"], 0, W))
                load(s_cols[W * d:W * d + W, 1:2], col(A["L0_attn_ln1_b"], 0, W))
                load(s_cols[W * d:W * d + W, 5:6], col(A["L0_attn_ln2_b"], 0, W))
                load(s_cols[:, 2 + d:3 + d], col(A["L0_attn_bx"], P * d, P))
                load(s_cols[:, 6 + d:7 + d], col(A["L0_attn_b1"], P * d, P))
            load(s_w2, A["L0_attn_W2"].rearrange("(f p) c -> p f c", p=P))
            load(s_fo, A["L0_ffn_Wo"])
            load(bi_col[:, :], col(A["L0_ffn_bi"], 0, P))
            load(route[:, :], A["L0_ffn_route_id"].unsqueeze(0))
            assert n_in[0] == WEIGHT_LOADS, n_in[0]

            for l in range(LAYERS):
                if l == 1:
                    sp.wait_ge(prep_dve, PREP_DVE)
                    sp.wait_ge(prep_mm, PREP_MM)
                sp.dma_start(e_nat[l], A["L0_ffn_Wr"][l].rearrange("e o k -> o e k")).then_inc(h1_dma[l], 16)
                sp.dma_start(e_ws[:, l, :], A["L0_ffn_Ws"][l, 0]).then_inc(experts_in, 16)
                sp.dma_start(e_b[EXPERTS * l:EXPERTS * l + EXPERTS, 0, :], A["L0_ffn_br"][l]).then_inc(experts_in, 16)
                sp.dma_start(e_b[EXPERTS * l:EXPERTS * l + EXPERTS, 1, :],
                             A["L0_ffn_bs"][l].to_broadcast([EXPERTS, HID])).then_inc(experts_in, 16)

            def experts():
                ewd = expert_w.rearrange("e p k -> p e k")
                sp.wait_ge(turned_in, 9)
                for l in range(LAYERS):
                    sp.dma_start(ewd[:, :, l * HID:(l + 1) * HID], e_turn[l]).then_inc(experts_out, 16)
                sp.dma_start(ewd[:, :, LAYERS * HID:EW], e_bT[:, :, :]).then_inc(experts_out, 16)
                sp.wait_ge(experts_out, 48)
                sp.wait_ge(weights_in, 16 * WEIGHT_LOADS)

            def load_image(im):
                if isinstance(im.i, int) and im.i == 0:
                    return
                bank_a.full(sp, before(im), "conv", CHUNKS - 1)
                after(sp, regrouped, RG * im.i)
                load_x(im)

            def fetch(im, s):
                if s >= WE_RING:
                    bank_c.taken(sp, im, "e2", s - WE_RING)
                n = SEGS * im.i + s
                e = sp.value_load(route[0:1, bass.ds(n, 1)], min_val=0, max_val=EXPERTS - 1)
                sp.dma_start(ew[:, s % WE_RING, :], expert_w[e]).then_inc(ew_in[s % WE_RING], 16)

            def ffn(im, t):
                if t == 0:
                    for s in range(WE_RING):
                        fetch(im, s)
                elif 3 <= t <= SEGS - 2:
                    fetch(im, t + 1)

            def store(im, c):
                bank_c.taken(sp, im, "out", c)
                o = out[im.i].rearrange("(c hh t) w -> hh c (t w)", hh=2, t=HR)
                for hh in range(2):
                    sp.dma_start(o[hh, :, CW * c:CW * c + CW],
                                 h1[im.p][CH * hh:CH * hh + CH, CW * c:CW * c + CW]).then_inc(h1_dma[im.p], 16)

            slots(sp, {"load": load_image, "ffn": ffn, "out": store}, experts=experts)
            for p in range(2):
                sp.wait_ge(h1_dma[p], 16 + 16 * 2 * CHUNKS * (IMAGES // 2))

        @block.gpsimd
        def _(pool):
            for k, v in ((HALF, 0.5), (QUARTER, 0.25), (PER_W, 1.0 / W), (EPSILON, EPS)):
                pool.memset(factor[:, k, :], v)
            pool.memset(neg_half[:, :], -0.5).then_inc(pow_done, 1)
            pool.wait_ge(pow_done, 1)
            pool.wait_ge(var_eps, 1)
            pool.tensor_tensor(s_cp[:, 6:7], s_cp[:, 5:6], neg_half[0:Y_HI_ROWS, 0:1], ALU.pow).then_inc(pow_done, 1)

            def statistics(kind, im):
                b, s, k, per_image = bn[kind], st[kind], [0], LN_STEPS[kind]
                me, mo, ve, vo = b[:, :, 1], b[:, :, 4], b[:, :, 2], b[:, :, 5]

                def link(ins):
                    k[0] += 1
                    ins.then_inc(ln_step[kind], 1)
                    pool.wait_ge(ln_step[kind], per_image * im.i + k[0])

                pool.wait_ge(bn_done[kind], CHUNKS * im.i + CHUNKS)
                link(pool.tensor_tensor(s[:, 1, :], me, mo, ALU.add))
                link(pool.tensor_tensor(s[:, 2, :], me, mo, ALU.subtract))
                link(pool.tensor_tensor(s[:, 3, :], ve, vo, ALU.add))
                link(pool.tensor_tensor(s[:, 0, :], s[:, 1, :], factor[:, HALF, :], ALU.mult))
                link(pool.tensor_tensor(s[:, 4, :], s[:, 2, :], s[:, 2, :], ALU.mult))
                link(pool.tensor_tensor(s[:, 4, :], s[:, 4, :], factor[:, QUARTER, :], ALU.mult))
                link(pool.tensor_tensor(s[:, 3, :], s[:, 3, :], factor[:, PER_W, :], ALU.mult))
                link(pool.tensor_tensor(s[:, 5, :], s[:, 3, :], s[:, 4, :], ALU.add))
                link(pool.tensor_tensor(s[:, 6, :], s[:, 5, :], factor[:, EPSILON, :], ALU.add))
                link(pool.tensor_tensor(s[:, 7, :], s[:, 6, :], neg_half[:, :], ALU.pow))
                return link, s, k

            def half(ap, g):
                return tiles(ap)[:, 16 * g:16 * g + 16, :]

            def spread(s, k, g):
                return s[:, k, 16 * g:16 * g + 16].unsqueeze(2).to_broadcast([P, 16, W])

            def norm0(im):
                link, s, k = statistics(0, im)
                link(pool.tensor_tensor(s[:, 4, :], s[:, 7, :], s[:, 7, :], ALU.mult))
                link(pool.tensor_tensor(s[:, 4, :], s[:, 4, :], s[:, 5, :], ALU.mult))
                link(pool.tensor_tensor(s[:, 4, :], s[:, 4, :], factor[:, EPSILON, :], ALU.add))
                link(pool.tensor_tensor(s[:, 6, :], s[:, 4, :], neg_half[:, :], ALU.pow))
                link(pool.tensor_tensor(s[:, 1, :], s[:, 6, :], s[:, 7, :], ALU.mult))
                for g in range(2):
                    link(pool.tensor_tensor(half(zn[:, :], g), half(h0[im.p][:, :], g), spread(s, 0, g), ALU.subtract))
                    after(pool, hi2, 2 * (im.i - 1) + g + 1)
                    after(pool, lo2, 2 * (im.i - 1) + g + 1)
                    pool.tensor_tensor(half(z[:, :], g), half(zn[:, :], g), spread(s, 7, g), ALU.mult).then_inc(z_ready, 1)
                assert k[0] == LN_STEPS[0]

            def norm2(im):
                link, s, k = statistics(2, im)
                for g in range(2):
                    pool.tensor_tensor(half(h0[im.p][:, :], g), half(h0[im.p][:, :], g), half(z[:, :], g),
                                       ALU.add).then_inc(s1_ready, 1)
                pool.wait_ge(s1_ready, 2 * im.i + 2)
                for g in range(2):
                    link(pool.tensor_tensor(half(z[:, :], g), half(z[:, :], g), spread(s, 0, g), ALU.subtract))
                    pool.tensor_tensor(half(z[:, :], g), half(z[:, :], g), spread(s, 7, g), ALU.mult).then_inc(n2_ready, 1)
                assert k[0] == LN_STEPS[2]

            def norm3(im):
                link, s, k = statistics(3, im)
                for g in range(2):
                    link(pool.tensor_tensor(half(n3[:, :], g), half(h1[im.p][:, :], g), spread(s, 0, g), ALU.subtract))
                    pool.tensor_tensor(half(n3[:, :], g), half(n3[:, :], g), spread(s, 7, g), ALU.mult).then_inc(n3_ready, 1)
                assert k[0] == LN_STEPS[3]

            slots(pool, {"norm0": norm0, "norm2": norm2, "norm3": norm3})

        @block.scalar
        def _(act):
            def conv(im, c):
                b = bank_a.full(act, im, "conv", c)
                act.activation(chunk(y16, c)[0:Y_HI_ROWS], psum[0:Y_HI_ROWS, b, :], ACT.Relu).then_inc(y_hi, 1)

            def patches(im, g):
                b = bank_a.full(act, im, "patches", g)
                act.activation(xpatch[:, g % 4, :, :], psum[0:PK, b, :].rearrange("p (a n) -> p a n", a=WP),
                               ACT.Copy).then_inc(freed[b], 1)

            def involve(im, c):
                b = bank_a.full(act, im, "involve", c)
                act.activation(chunk(h0[im.p], c), psum[:, b, :], ACT.Copy).then_inc(freed[b], 1)

            def zt(im, c):
                b = bank_a.full(act, im, "zt", c)
                act.activation(zT[:, c % 2, :], psum[:, b, :], ACT.Copy).then_inc(freed[b], 1)

            def logits(im, c):
                b = bank_a.full(act, im, "logits", c)
                act.activation(lg[:, TPC * c:TPC * c + TPC, :], psum[:, b, :].rearrange("p (t k) -> p t k", t=TPC),
                               ACT.Copy).then_inc(freed[b], 1)

            def kshift(im):
                act.wait_ge(q_step, Q_STEPS * im.i + 2)
                act.activation(lg[:, :, 0:HKR], lg[:, :, 0:HKR], ACT.Exp).then_inc(q_exp, 1)
                bank_a.taken(act, im, "kshift")
                act.activation(lg[:, :, HKR:2 * HKR], lg[:, :, HKR:2 * HKR], ACT.Exp).then_inc(k_exp, 1)

            def qt(im, j):
                b = bank_b.full(act, im, "qt", j)
                act.activation(qT[:, 4 * j:4 * j + 4, :], psum[:, b, :].rearrange("p (k n) -> p k n", k=4),
                               ACT.Copy).then_inc(freed[b], 1)

            def split2(im, g):
                act.wait_ge(n2_ready, 2 * im.i + (g + 1))
                act.activation(sp2[:, 16 * g:16 * g + 16, 0:W], tiles(z[:, :])[:, 16 * g:16 * g + 16, :],
                               ACT.Copy).then_inc(hi2, 1)

            def split3(im, g):
                act.wait_ge(n3_ready, 2 * im.i + (g + 1))
                act.activation(sp3[:, 16 * g:16 * g + 16, 0:W], tiles(n3[:, :])[:, 16 * g:16 * g + 16, :],
                               ACT.Copy).then_inc(hi3, 1)

            def w1(im, c, k):
                u, f = 2 * c + k // 2, k % 2
                b = bank_b.full(act, im, "w1", c, k)
                if f == 0:
                    after(act, ge_low, 2 * CHUNKS * im.i + u - 1)
                act.activation(gelu[:, u % 2, f, :], psum[:, b, :], ACT.Gelu,
                               bias=b1_col[:, f:f + 1]).then_inc(freed[b], 1)
                if f == 1:
                    bank_b.taken(act, im, "w1", c, k - 1)
                    bank_b.taken(act, im, "w1", c, k)
                    act.activation(ge_hi[:, u % 3, :, :], gelu[:, u % 2, :, :], ACT.Copy).then_inc(ge_high, 1)

            def ffn(im, t):
                if t < SEGS:
                    b = bank_c.full(act, im, "wi", t)
                    act.activation(hid_a[:, t % 2, :], psum[:, b, :], ACT.Relu, bias=bi_col[:, :]).then_inc(freed[b], 1)
                if 1 <= t <= SEGS:
                    s = t - 1
                    b = bank_c.full(act, im, "e1", s)
                    act.activation(hid_b[:, s % 2, :], psum[:, b, :], ACT.Relu,
                                   bias=ew[:, s % WE_RING, LAYERS * HID:LAYERS * HID + 1]).then_inc(freed[b], 1)
                if t >= 2:
                    s = t - 2
                    b = bank_c.full(act, im, "e2", s)
                    act.activation(hid_c[:, :, :, SEGC * s:SEGC * s + SEGC],
                                   psum[:, b, :].rearrange("p (t hh c) -> p t hh c", hh=2, c=SEGC), ACT.Relu,
                                   bias=ew[:, s % WE_RING, LAYERS * HID + 1:LAYERS * HID + 2]).then_inc(freed[b], 1)

            act.wait_ge(prep_dve, PREP_DVE)
            slots(act, {"conv": conv, "patches": patches, "involve": involve, "zt": zt, "logits": logits,
                        "kshift": kshift, "qt": qt, "split2": split2, "split3": split3, "w1": w1, "ffn": ffn})

        @block.vector
        def _(dve):
            chain = [0]

            def link(ins):
                chain[0] += 1
                ins.then_inc(prep_link, 1)
                dve.wait_ge(prep_link, chain[0])

            def done(ins):
                ins.then_inc(prep_dve, 1)

            link(dve.memset(xpad[:, :, :], 0.0))
            link(dve.memset(s_cw, 0.0))
            link(dve.memset(s_bdqk, 0.0))
            dve.memset(s_bdv, 0.0).then_inc(zeroed, 1)
            dve.memset(y16[Y_ONE_ROW:Y_ROWS, :], 1.0)
            dve.memset(ones3[:, :], 1.0)
            dve.memset(ones_col[:, :], 1.0)
            dve.memset(w1_l0[:, :], 0.0)
            dve.memset(wi_l0[:, :], 0.0)
            dve.memset(qk_w[:, :], 0.0)
            dve.memset(gmix[:, :, :], 0.0)
            for v in (head_w[:, :, :], khT[:, :], gT4[:, :, :]):
                dve.memset(v, 0.0)
            link(dve.memset(tap_w[:, :, :, :, :, :], 0.0))

            dve.wait_ge(weights_in, 16 * WEIGHT_LOADS)
            dve.tensor_scalar(s_cp[:, 5:6], s_cp[:, 4:5], EPS, None, ALU.add).then_inc(var_eps, 1)
            dve.wait_ge(pow_done, 2)
            link(dve.tensor_tensor(s_cp[:, 7:8], s_cp[:, 6:7], s_cp[:, 1:2], ALU.mult))
            link(dve.tensor_tensor(s_cp[:, 5:6], s_cp[:, 0:1], s_cp[:, 3:4], ALU.subtract))
            link(dve.tensor_tensor(s_cp[:, 5:6], s_cp[:, 5:6], s_cp[:, 7:8], ALU.mult))
            link(dve.tensor_tensor(s_cp[:, 5:6], s_cp[:, 5:6], s_cp[:, 2:3], ALU.add))
            link(dve.tensor_scalar(s_cw, s_cw, s_cp[:, 7:8], None, ALU.mult))
            done(dve.tensor_copy(s_cb3, s_cp[:, 5:6].to_broadcast([Y_HI_ROWS, 3])))

            dve.wait_ge(prep_mm, 1)
            dve.tensor_copy(s_wxT, psum[:, 0, 0:2 * W].rearrange("p (b w) -> p b w", b=2).unsqueeze(2)
                            .to_broadcast([P, 2, 2, W]))
            link(dve.tensor_tensor(s_cols[:, 8:10], psum[:, 1, 0:2], s_cols[:, 2:4], ALU.add))
            dve.tensor_copy(s_u3, s_cols[:, 8:10].unsqueeze(2).to_broadcast([P, 2, 3]))
            dve.tensor_tensor(b1_col[:, :], psum[:, 1, 2:4], s_cols[:, 6:8], ALU.add)
            dve.tensor_copy(fo_w[:, :], psum[:, 3, 0:W])
            dve.tensor_scalar(s_w1g, s_w1, s_cols[:, 4:5], None, ALU.mult)
            link(dve.tensor_copy(wi_hh[:, :], psum[:, 2, 0:HID]))
            dve.tensor_tensor(wi_l0[0:W, :], psum[0:W, 2, 0:HID], wi_hh[0:W, :], ALU.subtract)
            link(dve.tensor_copy(w1_hh[:, :], s_w1g))
            link(dve.tensor_copy(w2_hi[:, :, :], s_w2))
            dve.tensor_tensor(w2_lo[:, :, :], s_w2, w2_hi[:, :, :], ALU.subtract)
            done(dve.tensor_tensor(w1_l0[0:W, :], s_w1g[0:W, :], w1_hh[0:W, :], ALU.subtract))

            link(dve.tensor_copy(w2h16, s_w2f))
            link(dve.tensor_tensor(s_w2r, s_w2f, w2h16, ALU.subtract))
            link(dve.tensor_copy(w2m16, s_w2r))
            link(dve.tensor_tensor(w2l16, s_w2r, w2m16, ALU.subtract))
            for hh in range(2):
                link(dve.tensor_scalar(s_w2a[:, hh, :], w2h16, ypick[:, hh, 0:1], None, ALU.mult))
                link(dve.scalar_tensor_tensor(s_w2a[:, hh, :], w2m16, ypick[:, hh, 1:2], s_w2a[:, hh, :],
                                              ALU.mult, ALU.add))
                link(dve.scalar_tensor_tensor(s_w2a[:, hh, :], w2l16, ypick[:, hh, 2:3], s_w2a[:, hh, :],
                                              ALU.mult, ALU.add))
                link(dve.tensor_copy(w2d16[:, hh, :, :].rearrange("p i (d j) -> p i d j", d=2),
                                     s_w2a[:, hh, :].rearrange("p (i j) -> p i j", i=3).unsqueeze(2)
                                     .to_broadcast([Y_ROWS, 3, 2, 3])))
                for r in range(PR):
                    for k in range(3):
                        a = (3 - k) % 3
                        last = dve.tensor_copy(tap_w[:, hh, r, k, r:r + 3, :].rearrange("p i (n j) -> p i n j", j=3),
                                               w2d16[:, hh, :, a:a + 3].unsqueeze(2).to_broadcast([Y_ROWS, 3, 6, 3]))
            link(last)

            dve.wait_ge(prep_mm, 2)
            dve.tensor_copy(conv_w[:, :], psum[:, 4, 0:Y_HI_ROWS])
            dve.tensor_copy(s_brf[:, B_CONV:B_CONV + Y_HI_ROWS], psum[0:3, 5, 0:Y_HI_ROWS])
            dve.wait_ge(prep_mm, 3)
            for b in range(2):
                dve.tensor_copy(s_brf[:, B_QK:B_QK + 2 * HKR].rearrange("p (a b n) -> p a b n", a=2, b=2)[:, :, b, :],
                                psum[0:3, 7, 32 * b:32 * b + 32].rearrange("p (a n) -> p a n", a=2))
                for d in range(2):
                    rows = slice(W * d, W * d + W)
                    dve.tensor_scalar(
                        qk_w[rows, 64 * d:64 * d + 64].rearrange("p (a b n) -> p a b n", a=2, b=2)[:, :, b, :],
                        psum[rows, 6, 32 * b:32 * b + 32].rearrange("p (a n) -> p a n", a=2),
                        s_cols[rows, 0:1], None, ALU.mult)
            dve.tensor_copy(s_vxT, psum[:, 0, 0:2 * W].rearrange("p (b w) -> p b w", b=2))
            link(dve.tensor_copy(s_cols[:, 10:12], psum[:, 1, 0:2]))
            for b in range(2):
                dve.tensor_scalar(s_vbx[:, b, :], headcols[:, b, :], s_cols[:, 10 + b:11 + b], None, ALU.mult)
                dve.tensor_tensor(s_wom[:, b, :, :], s_wo[:, b, :].unsqueeze(1).to_broadcast([P, 4, W]),
                                  headrows[:, :].unsqueeze(2).to_broadcast([P, 4, W]), ALU.mult)
            link(dve.tensor_copy(brh, s_brf))
            link(dve.tensor_tensor(s_brr, s_brf, brh, ALU.subtract))
            link(dve.tensor_copy(brm, s_brr))
            link(dve.tensor_tensor(brl, s_brr, brm, ALU.subtract))
            link(dve.tensor_scalar(s_bra, brh, ident[0:3, 0:1], None, ALU.mult))
            link(dve.scalar_tensor_tensor(s_bra, brm, ident[0:3, 1:2], s_bra, ALU.mult, ALU.add))
            done(dve.scalar_tensor_tensor(bias_rows[:, :], brl, ident[0:3, 2:3], s_bra, ALU.mult, ALU.add))

            dve.wait_ge(prep_mm, 4)
            for b in range(2):
                dve.tensor_scalar(head_w[0:W, 4 * b:4 * b + 4, :],
                                  psum[0:W, 2 + b, 0:4 * W].rearrange("p (h c) -> p h c", h=4),
                                  s_cols[0:W, 0:1], None, ALU.mult)
            done(dve.tensor_copy(head_b[:, :], psum[:, 4, 0:W]))

            def experts():
                dve.wait_ge(experts_in, 16 * 3 * LAYERS)
                for l in range(LAYERS):
                    dve.wait_ge(h1_dma[l], 16)
                    link(dve.tensor_tensor(e_ws[:, l, :], e_ws[:, l, :], ident[:, :], ALU.add))
                    v = e_nat[l]
                    dve.tensor_tensor(v, v, e_ws[:, l, :].unsqueeze(1).to_broadcast([P, EXPERTS, HID]),
                                      ALU.add).then_inc(experts_sum, 1)
                dve.tensor_tensor(e_b[:, 0, :], e_b[:, 0, :], e_b[:, 1, :], ALU.add).then_inc(experts_sum, 1)
                for n in range(8):
                    dve.wait_ge(turned, n + 1)
                    dve.tensor_copy(e_turn[n // 4][:, 4 * (n % 4):4 * (n % 4) + 4, :],
                                    psum[:, 6 + n % 2, :].rearrange("p (e k) -> p e k", e=4)).then_inc(turned_in, 1)
                dve.wait_ge(turned, 9)
                dve.tensor_copy(e_bT[:, :, :].rearrange("p e l -> p l e"),
                                psum[:, 6, 0:LAYERS * EXPERTS].rearrange("p (l e) -> p l e", l=LAYERS)
                                ).then_inc(turned_in, 1)

            def conv(im, c):
                dve.wait_ge(y_hi, CHUNKS * im.i + (c + 1))
                b = bank_a.full(dve, im, "conv", c)
                lo = chunk(y16, c)[Y_LO_ROW:Y_HI_ROWS]
                dve.scalar_tensor_tensor(lo, psum[Y_LO_ROW:Y_HI_ROWS, b, :], 0.0, lo, ALU.max,
                                         ALU.subtract).then_inc(freed[b], 1)

            def regroup(im, g):
                if g == 0:
                    dve.wait_ge(x_in, 32 * im.i + 32)
                if g >= 4:
                    bank_a.full(dve, im, "patches", g - 4)
                else:
                    bank_a.full(dve, before(im), "patches", g + 4)
                rows = xpad[:, PR * g:PR * g + PR + 2, :]
                src = bass.AP(rows.tensor, rows.offset, [rows.ap[0], [PW, WP], rows.ap[1], [1, PW + 2]])
                dve.tensor_copy(xrun[:, g % 4, :, :, :], src).then_inc(regrouped, 1)

            def filters(im, hh, r):
                b = bank_a.full(dve, im, "filters", hh, r)
                dve.tensor_tensor(filt[hh].rearrange("p (g r w) -> p g r w", r=PR, w=W)[:, :, r, :],
                                  psum[0:PK, b, :].rearrange("p (g w) -> p g w", w=W),
                                  bandmask[:, :].unsqueeze(1).to_broadcast([PK, RG, W]), ALU.mult).then_inc(freed[b], 1)

            def stats(kind, ap, c):
                for t in range(TPC * c, TPC * c + TPC):
                    ins = dve.bn_stats(bn[kind][:, t, :], ap[:, W * t:W * t + W])
                ins.then_inc(bn_done[kind], 1)

            def involve(im, c):
                bank_a.taken(dve, im, "involve", c)
                stats(0, h0[im.p], c)

            def scale(im, g):
                dve.wait_ge(z_ready, 2 * im.i + (g + 1))
                v = tiles(zn[:, :])[:, 16 * g:16 * g + 16, :]
                dve.tensor_tensor(v, v, st[0][:, 1, 16 * g:16 * g + 16].unsqueeze(2).to_broadcast([P, 16, W]),
                                  ALU.mult).then_inc(zn_ready, 1)

            def kmax(im):
                bank_a.taken(dve, im, "logits", CHUNKS - 1)
                dve.tensor_reduce(kmx[:, :], lg[:, :, HKR:2 * HKR].rearrange("p t k -> p k t"), AX.X,
                                  ALU.max).then_inc(k_step, 1)
                ql = lg[:, :, 0:HKR].rearrange("p t (h r) -> p t h r", r=KR)
                dve.tensor_reduce(qmx[:, :, :], ql, AX.X, ALU.max).then_inc(q_step, 1)
                dve.wait_ge(q_step, Q_STEPS * im.i + 1)
                dve.tensor_tensor(ql, ql, qmx[:, :, :].unsqueeze(3).to_broadcast([P, HR, HEADS, KR]),
                                  ALU.subtract).then_inc(q_step, 1)

            def kshift(im):
                b = bank_a.full(dve, im, "kmax")
                dve.tensor_reduce(kmc[:, :], psum[0:HKR, b, 0:P], AX.X, ALU.max).then_inc(k_step, 1)
                dve.wait_ge(k_step, K_STEPS * im.i + 2)
                dve.tensor_copy(kmb[:, :], kmc[:, :].to_broadcast([HKR, P])).then_inc(freed[b], 1)
                b = bank_a.full(dve, im, "kshift")
                kl = lg[:, :, HKR:2 * HKR]
                dve.tensor_tensor(kl, kl, psum[:, b, 0:HKR].unsqueeze(1).to_broadcast([P, HR, HKR]),
                                  ALU.subtract).then_inc(freed[b], 1)

            def pool(im):
                ql = lg[:, :, 0:HKR].rearrange("p t (h r) -> p t h r", r=KR)
                dve.wait_ge(q_exp, im.i + 1)
                dve.tensor_reduce(qden[:, :, :], ql, AX.X, ALU.add).then_inc(q_step, 1)
                dve.wait_ge(q_step, Q_STEPS * im.i + 3)
                dve.reciprocal(qinv[:, :, :], qden[:, :, :]).then_inc(q_step, 1)
                dve.wait_ge(k_exp, im.i + 1)
                dve.tensor_reduce(kmx[:, :], lg[:, :, HKR:2 * HKR].rearrange("p t k -> p k t"), AX.X,
                                  ALU.add).then_inc(k_step, 1)
                dve.wait_ge(k_step, K_STEPS * im.i + 3)
                dve.tensor_copy(ksum[:, :, :], kmx[:, :].unsqueeze(1).to_broadcast([P, 4, HKR])).then_inc(k_step, 1)
                dve.wait_ge(q_step, Q_STEPS * im.i + 4)
                dve.tensor_tensor(q[:, :, :].rearrange("p t (h r) -> p t h r", r=KR), ql,
                                  qinv[:, :, :].unsqueeze(3).to_broadcast([P, HR, HEADS, KR]),
                                  ALU.mult).then_inc(q_step, 1)

            def mix(im):
                b = bank_a.full(dve, im, "pool")
                dve.reciprocal(kinv[:, :], psum[:, b, 64:65]).then_inc(k_step, 1)
                dve.tensor_copy(khT[0:W, :], psum[0:W, b, 0:HKR]).then_inc(freed[b], 1)

            def mixt(im):
                b = bank_a.full(dve, im, "mix")
                dve.tensor_copy(gT4[0:W, :, :], psum[0:W, b, 0:HKR].unsqueeze(1).to_broadcast([W, 4, HKR])
                                ).then_inc(freed[b], 1)
                b = bank_a.full(dve, im, "mixt")
                dve.wait_ge(k_step, K_STEPS * im.i + 5)
                for k in range(4):
                    rows = slice(HKR * k, HKR * k + HKR)
                    ins = dve.scalar_tensor_tensor(gmix[rows, k, :], psum[rows, b, 0:W], kinv[rows, :],
                                                   head_b[rows, :], ALU.mult, ALU.add)
                ins.then_inc(freed[b], 1)

            def attend(im, c):
                b = bank_b.full(dve, im, "attend", c)
                if c == 0:
                    dve.wait_ge(z_ready, 2 * im.i + 2)
                dve.tensor_tensor(chunk(z, c), psum[:, b, :], chunk(z, c), ALU.add).then_inc(freed[b], 1)
                if c > 0:
                    bank_b.taken(dve, im, "attend", c - 1)
                    stats(2, z, c - 1)
                if c == CHUNKS - 1:
                    bank_b.taken(dve, im, "attend", c)
                    stats(2, z, c)

            def split2(im, g):
                dve.wait_ge(hi2, 2 * im.i + (g + 1))
                t = slice(16 * g, 16 * g + 16)
                dve.tensor_tensor(sp2[:, t, W:2 * W], tiles(z[:, :])[:, t, :], sp2[:, t, 0:W],
                                  ALU.subtract).then_inc(lo2, 1)

            def split3(im, g):
                dve.wait_ge(hi3, 2 * im.i + (g + 1))
                t = slice(16 * g, 16 * g + 16)
                dve.tensor_tensor(sp3[:, t, W:2 * W], tiles(n3[:, :])[:, t, :], sp3[:, t, 0:W],
                                  ALU.subtract).then_inc(lo3, 1)

            def ft(im, c):
                b = bank_b.full(dve, im, "ft", c)
                dve.tensor_copy(fT[:, c % 2, :], psum[:, b, :].bitcast(F16)).then_inc(freed[b], 1)

            def z3t(im, c):
                b = bank_c.full(dve, im, "z3t", c)
                dve.tensor_copy(z3T[:, TPC * c:TPC * c + TPC, :, :].rearrange("p t hh c -> p (t hh c)"),
                                psum[:, b, :].bitcast(F16)).then_inc(freed[b], 1)

            def w1(im, c, k):
                if k % 2:
                    u = 2 * c + k // 2
                    dve.wait_ge(ge_high, 2 * CHUNKS * im.i + (u + 1))
                    dve.tensor_tensor(ge_lo[:, u % 3, :, :], gelu[:, u % 2, :, :], ge_hi[:, u % 3, :, :],
                                      ALU.subtract).then_inc(ge_low, 1)

            def w2(im, c, k):
                if k < 3:
                    return
                b = bank_m.full(dve, im, "w2", c)
                if c == 0:
                    dve.wait_ge(s1_ready, 2 * im.i + 2)
                    dve.wait_ge(h1_dma[im.p], 16 + 16 * 2 * CHUNKS * im.h)
                dve.tensor_tensor(chunk(h1[im.p], c), psum[:, b, :], chunk(h0[im.p], c), ALU.add).then_inc(freed[b], 1)
                bank_m.taken(dve, im, "w2", c)
                stats(3, h1[im.p], c)

            def add_ffn(im, c):
                b = bank_c.full(dve, im, "out", c)
                v = chunk(h1[im.p], c)
                dve.tensor_tensor(v, psum[:, b, :], v, ALU.add).then_inc(freed[b], 1)

            slots(dve, {"conv": conv, "regroup": regroup, "filters": filters, "involve": involve, "scale": scale, "kmax": kmax,
                        "kshift": kshift, "pool": pool, "mix": mix, "mixt": mixt, "attend": attend, "split2": split2,
                        "split3": split3, "ft": ft, "z3t": z3t, "w1": w1, "w2": w2,
                        "out": add_ffn}, experts=experts)

        @block.tensor
        def _(pe):
            pe.wait_ge(weights_in, 16 * WEIGHT_LOADS)
            pe.wait_ge(zeroed, 1)
            for b in range(2):
                cols = slice(P * b, P * b + P)
                pe.transpose(psum[:, 0, W * b:W * b + W], s_wx[:, cols], ident[0:W, 0:W])
                pe.matmul(psum[:, 1, b:b + 1], s_wx[:, cols], s_cols[0:W, 1:2], start=True, stop=True)
                pe.matmul(psum[:, 1, 2 + b:3 + b], s_w1[0:W, cols], s_cols[0:W, 5:6], start=True, stop=True)
            pe.transpose(psum[:, 2, 0:HID], s_wi.rearrange("p d w -> p (d w)"), ident[:, :])
            pe.transpose(psum[:, 3, 0:W], s_fo, ident[0:W, 0:W]).then_inc(prep_mm, 1)

            pe.wait_ge(prep_dve, 1)
            pe.transpose(psum[:, 4, 0:Y_HI_ROWS], s_cw, ident[0:Y_HI_ROWS, 0:Y_HI_ROWS])
            pe.transpose(psum[0:3, 5, 0:Y_HI_ROWS], s_cb3, ident[0:Y_HI_ROWS, 0:Y_HI_ROWS]).then_inc(prep_mm, 1)

            pe.wait_ge(prep_dve, 2)
            for b in range(2):
                pe.matmul(psum[:, 6, 32 * b:32 * b + 32], s_wxT[:, b, :, :].rearrange("p d w -> p (d w)"), s_bdqk,
                          start=True, stop=True)
                pe.matmul(psum[0:3, 7, 32 * b:32 * b + 32], s_u3[:, b, :], s_bdqk, start=True, stop=True)
                pe.matmul(psum[:, 0, W * b:W * b + W], s_bdv, s_wxT[:, b, 0, :], start=True, stop=True)
                mm = pe.matmul(psum[:, 1, b:b + 1], s_bdv, s_cols[:, 8 + b:9 + b], start=True, stop=True)
            mm.then_inc(prep_mm, 1)

            pe.wait_ge(prep_dve, 3)
            for b in range(2):
                pe.matmul(psum[0:W, 2 + b, 0:4 * W], s_vxT[:, b, :], s_wom[:, b, :, :], start=True, stop=True)
            for b in range(2):
                mm = pe.matmul(psum[:, 4, 0:W], s_vbx[:, b, :], s_wo[:, b, :], start=(b == 0), stop=(b == 1))
            mm.then_inc(prep_mm, 1)
            pe.wait_ge(prep_dve, PREP_DVE)

            def experts():
                for n in range(8):
                    pe.wait_ge(experts_sum, n // 4 + 1)
                    if n >= 2:
                        pe.wait_ge(turned_in, n - 1)
                    for k in range(4):
                        mm = pe.transpose(psum[:, 6 + n % 2, HID * k:HID * k + HID], e_nat[n // 4][:, 4 * (n % 4) + k, :],
                                          ident[:, :])
                    mm.then_inc(turned, 1)
                pe.wait_ge(experts_sum, 3)
                pe.wait_ge(turned_in, 7)
                pe.transpose(psum[:, 6, 0:LAYERS * EXPERTS], e_b[:, 0, :], ident[0:32, 0:32]).then_inc(turned, 1)
                pe.wait_ge(turned_in, 9)

            def bias(b, a, n, reps):
                pe.matmul(psum[:, b, :], ones3[:, 0:P], bias_rows[:, a:a + n].unsqueeze(1).to_broadcast([3, reps, n]),
                          start=True, stop=False, skip_group_check=True)

            def conv(im, c):
                if c == 0:
                    pe.wait_ge(x_in, 32 * im.i + 32)
                b = bank_a.claim(pe, im, "conv", c)
                pe.matmul(psum[0:Y_HI_ROWS, b, :], bias_rows[:, B_CONV:B_CONV + Y_HI_ROWS], ones3[:, :], start=True,
                          stop=False)
                pe.matmul(psum[0:Y_HI_ROWS, b, :], conv_w[:, :], xpad[:, 1 + TPC * c:1 + TPC * c + TPC, 1:W + 1],
                          start=False, stop=True).then_inc(filled[b], 1)

            def filters(im, hh, r):
                b = bank_a.claim(pe, im, "filters", hh, r,
                                 needs=[("conv", c) for c in range(CHUNKS)] if (hh, r) == (0, 0) else [])
                y = y16[:, :].rearrange("p (g r a w) -> p g r a w", r=PR, a=WP, w=PW)[:, :, r, :, :]
                o = psum[0:PK, b, :].rearrange("p (g a w) -> p g a w", a=WP, w=PW)
                for k in range(3):
                    mm = pe.matmul(o[:, :, :, k::3], tap_w[:, hh, r, k, :, :].rearrange("p i j -> p (i j)"),
                                   y[:, :, :, k::3], start=True, stop=True)
                mm.then_inc(filled[b], 1)

            def patches(im, g):
                b = bank_a.claim(pe, im, "patches", g)
                pe.wait_ge(regrouped, RG * im.i + (g + 1))
                for a in range(WP):
                    mm = pe.transpose(psum[0:PK, b, P * a:P * a + P],
                                      xrun[:, g % 4, a, :, :].rearrange("p i j -> p (i j)"), ident[:, :])
                mm.then_inc(filled[b], 1)

            def involve(im, c):
                needs = [("patches", 2 * c)]
                if c == 0:
                    needs += [("filters", hh, r) for hh in range(2) for r in range(PR)]
                b = bank_a.claim(pe, im, "involve", c, needs=needs)
                for g in (2 * c, 2 * c + 1):
                    if g % 2:
                        bank_a.taken(pe, im, "patches", g)
                    for a in range(WP):
                        for hh in range(2):
                            rows = slice(CH * hh, CH * hh + CH)
                            o = psum[rows, b, 256 * (g % 2):256 * (g % 2) + 256].rearrange("p (r w) -> p r w", w=W)
                            f = filt[hh].rearrange("p (t w) -> p t w", w=W)
                            mm = pe.matmul(o[:, :, PW * a:PW * a + PW], xpatch[:, g % 4, a, rows],
                                           f[:, PR * g:PR * g + PR, PW * a:PW * a + PW], start=True, stop=True)
                mm.then_inc(filled[b], 1)

            def zt(im, c):
                if c % 2 == 0:
                    pe.wait_ge(zn_ready, 2 * im.i + (c // 2 + 1))
                b = bank_a.claim(pe, im, "zt", c)
                for k in range(4):
                    n = CW * c + P * k
                    mm = pe.transpose(psum[:, b, P * k:P * k + P], zn[:, n:n + P], ident[:, :])
                mm.then_inc(filled[b], 1)

            def logits(im, c):
                b = bank_a.claim(pe, im, "logits", c, needs=[("zt", c)])
                bias(b, B_QK, 2 * HKR, TPC)
                for k in range(4):
                    mm = pe.matmul(psum[:, b, P * k:P * k + P], zT[:, c % 2, P * k:P * k + P], qk_w[:, :],
                                   start=False, stop=True, skip_group_check=True)
                mm.then_inc(filled[b], 1)

            def kmax(im):
                b = bank_a.claim(pe, im, "kmax")
                pe.wait_ge(k_step, K_STEPS * im.i + 1)
                pe.transpose(psum[0:HKR, b, 0:P], kmx[:, :], ident[:, :]).then_inc(filled[b], 1)

            def kshift(im):
                b = bank_a.claim(pe, im, "kshift", needs=[("kmax",)])
                pe.matmul(psum[:, b, 0:HKR], kmb[:, :], ident[0:HKR, 0:HKR], start=True, stop=True).then_inc(filled[b], 1)

            def pool(im):
                b = bank_a.claim(pe, im, "pool")
                pe.wait_ge(k_exp, im.i + 1)
                for t in range(HR):
                    pe.matmul(psum[0:W, b, 0:HKR], zn[:, W * t:W * t + W], lg[:, t, HKR:2 * HKR], start=(t == 0),
                              stop=(t == HR - 1))
                pe.wait_ge(k_step, K_STEPS * im.i + 4)
                pe.matmul(psum[:, b, 64:65], ksum[:, :, :].rearrange("p a k -> p (a k)"), ones_col[:, :], start=True,
                          stop=True).then_inc(filled[b], 1)

            def mix(im):
                b = bank_a.claim(pe, im, "mix", needs=[("pool",)])
                for h in range(HEADS):
                    mm = pe.matmul(psum[0:W, b, KR * h:KR * h + KR], head_w[:, h, :], khT[:, KR * h:KR * h + KR],
                                   start=True, stop=True)
                mm.then_inc(filled[b], 1)

            def mixt(im):
                b = bank_a.claim(pe, im, "mixt", needs=[("mix",)])
                pe.transpose(psum[:, b, 0:P], gT4[:, :, :].rearrange("p a k -> p (a k)"), ident[:, :]
                             ).then_inc(filled[b], 1)

            def qt(im, j):
                if j == 0:
                    pe.wait_ge(q_step, Q_STEPS * im.i + Q_STEPS)
                b = bank_b.claim(pe, im, "qt", j)
                for k in range(4):
                    t = 16 * j + 4 * k
                    mm = pe.transpose(psum[:, b, P * k:P * k + P], q[:, t:t + 4, :].rearrange("p t k -> p (t k)"),
                                      ident[:, :])
                mm.then_inc(filled[b], 1)

            def attend(im, c):
                b = bank_b.claim(pe, im, "attend", c, needs=[("qt", c // 2)])
                if c == 0:
                    bank_a.taken(pe, im, "mixt")
                bias(b, B_ATT, W, TPC)
                for k in range(2):
                    mm = pe.matmul(psum[:, b, 256 * k:256 * k + 256], qT[:, 2 * c + k, :],
                                   gmix[:, :, :].rearrange("p k w -> p (k w)"), start=False, stop=True,
                                   skip_group_check=True)
                mm.then_inc(filled[b], 1)

            def turn16(b, src, c):
                o = psum[:, b, :].bitcast(F16)
                for k in range(TPC):
                    mm = pe.transpose(o[:, P * k:P * k + P], src[:, TPC * c + k, :], ident16[:, :])
                mm.then_inc(filled[b], 1)

            def ft(im, c):
                if c % 2 == 0:
                    pe.wait_ge(lo2, 2 * im.i + (c // 2 + 1))
                turn16(bank_b.claim(pe, im, "ft", c), sp2, c)

            def z3t(im, c):
                if c % 2 == 0:
                    pe.wait_ge(lo3, 2 * im.i + (c // 2 + 1))
                turn16(bank_c.claim(pe, im, "z3t", c), sp3, c)

            def w1(im, c, k):
                b = bank_b.claim(pe, im, "w1", c, k, needs=[("ft", c)])
                f, x = slice(P * (k % 2), P * (k % 2) + P), fT[:, c % 2, 512 * (k // 2):512 * (k // 2) + 512]
                pe.matmul(psum[:, b, :], w1_hh[:, f], x, start=True, stop=False)
                pe.matmul(psum[:, b, :], w1_l0[:, f], x, start=False, stop=True).then_inc(filled[b], 1)

            def w2(im, c, k):
                if k == 0:
                    bias(bank_m.claim(pe, im, "w2", c), B_MLP, W, TPC)
                b = bank_m.place["w2", c][0]
                u = 2 * c + k // 2
                if k % 2 == 0:
                    pe.wait_ge(ge_low, 2 * CHUNKS * im.i + (u + 1))
                for t in (2 * k, 2 * k + 1):
                    n = P * (t % 4)
                    for f in range(2):
                        for g, w in ((ge_hi, w2_hi), (ge_hi, w2_lo), (ge_lo, w2_hi)):
                            mm = pe.matmul(psum[:, b, W * t:W * t + W], g[:, u % 3, f, n:n + P], w[:, f, :],
                                           start=False, stop=(f == 1 and g is ge_lo), skip_group_check=True)
                if k == 3:
                    mm.then_inc(filled[b], 1)

            def ffn(im, t):
                if t < SEGS:
                    b = bank_c.claim(pe, im, "wi", t, needs=[("z3t", c) for c in range(CHUNKS)])
                    x = z3T[:, :, :, SEGC * t:SEGC * t + SEGC]
                    pe.matmul(psum[:, b, :], wi_hh[:, :], x, start=True, stop=False)
                    pe.matmul(psum[:, b, :], wi_l0[:, :], x, start=False, stop=True).then_inc(filled[b], 1)
                if 1 <= t <= SEGS:
                    s = t - 1
                    b = bank_c.claim(pe, im, "e1", s, needs=[("wi", s)])
                    pe.wait_ge(ew_in[s % WE_RING], 16 * (SEGS // WE_RING) * im.i + 16 * (s // WE_RING + 1))
                    pe.matmul(psum[:, b, :], ew[:, s % WE_RING, 0:HID], hid_a[:, s % 2, :], start=True,
                              stop=True).then_inc(filled[b], 1)
                if t >= 2:
                    s = t - 2
                    b = bank_c.claim(pe, im, "e2", s, needs=[("e1", s)])
                    pe.matmul(psum[:, b, :], ew[:, s % WE_RING, HID:2 * HID], hid_b[:, s % 2, :], start=True,
                              stop=True).then_inc(filled[b], 1)

            def ffn_out(im, c):
                b = bank_c.claim(pe, im, "out", c, needs=[("e2", s) for s in range(SEGS)])
                bias(b, B_FFN, W, TPC)
                for k in range(TPC):
                    mm = pe.matmul(psum[:, b, W * k:W * k + W],
                                   hid_c[:, TPC * c + k, :, :].rearrange("p hh c -> p (hh c)"), fo_w[:, :], start=False,
                                   stop=True, skip_group_check=True)
                mm.then_inc(filled[b], 1)

            slots(pe, {"conv": conv, "filters": filters, "patches": patches, "involve": involve, "zt": zt,
                       "logits": logits, "kmax": kmax, "kshift": kshift, "pool": pool, "mix": mix, "mixt": mixt,
                       "qt": qt, "attend": attend, "ft": ft, "z3t": z3t, "w1": w1, "w2": w2, "ffn": ffn,
                       "out": ffn_out}, experts=experts)


_INS = ["x", "L0_tok_conv1_w", "L0_tok_conv1_b", "L0_tok_bn_gamma", "L0_tok_bn_beta", "L0_tok_bn_mean",
        "L0_tok_bn_var", "L0_tok_conv2_w", "L0_tok_conv2_b", "L0_attn_ln1_g", "L0_attn_ln1_b", "L0_attn_Wx",
        "L0_attn_bx", "L0_attn_Wq", "L0_attn_Wk", "L0_attn_Wv", "L0_attn_Wo", "L0_attn_bo", "L0_attn_ln2_g",
        "L0_attn_ln2_b", "L0_attn_W1", "L0_attn_b1", "L0_attn_W2", "L0_attn_b2", "L0_ffn_route_id", "L0_ffn_Wi",
        "L0_ffn_bi", "L0_ffn_Wr", "L0_ffn_br", "L0_ffn_Ws", "L0_ffn_bs", "L0_ffn_Wo", "L0_ffn_bo"]


def constants():
    eye = np.eye(P, dtype=np.float32)
    band = np.zeros((PR + 2, PW + 2, WP, PW), np.float32)
    for w in range(PW):
        band[:, w:w + 3, :, w] = 1
    head = np.arange(P) // DH
    cols = np.tile(np.repeat(np.arange(HEADS), KR), 4)
    headcols = np.stack([(4 * b + head)[:, None] == cols[None, :] for b in range(2)], 1).astype(np.float32)
    headrows = (head[:, None] == np.arange(4)[None, :]).astype(np.float32)
    ypick = np.zeros((Y_ROWS, 2, 3), np.float32)
    for g, (hh, part) in enumerate(((0, 0), (0, 1), (1, 0), (1, 1), (0, 0), (1, 0))):
        ypick[CR * g:CR * g + CR, hh, part] = 1
    for part in range(3):
        ypick[Y_ONE_ROW + part, :, part] = 1
    return {"k_ident": eye, "k_ident16": eye.astype(np.float16), "k_bandmask": band.reshape(PK, W),
            "k_headcols": headcols, "k_headrows": headrows, "k_ypick": ypick}


def kernel(**inputs):
    import concourse.bacc as _bacc
    from concourse.bass_utils import run_bass_kernel_spmd as _run

    nc = _bacc.Bacc("TRN2", target_bir_lowering=False, num_devices=1)
    arrays, args = {}, {}
    for name, a in [(n, inputs[n]) for n in _INS] + list(constants().items()):
        a = np.ascontiguousarray(a)
        arrays[f"in_{name}"] = a
        args[name] = nc.dram_tensor(f"in_{name}", a.shape, mybir.dt.from_np(a.dtype), kind="ExternalInput").ap()
    out = nc.dram_tensor("out_0", (IMAGES, CH * ROWS, W), F32, kind="ExternalOutput").ap()
    tower_kernel(nc, args, out)
    r = _run(nc, [arrays], core_ids=[0])
    return r.results[0]["out_0"]
```

```python
from contextlib import ExitStack
from collections import namedtuple

import numpy as np
import concourse.bass as bass
from concourse import mybir

F32, F16, BF16, I32 = mybir.dt.float32, mybir.dt.float16, mybir.dt.bfloat16, mybir.dt.int32
ALU = mybir.AluOpType
ACT = mybir.ActivationFunctionType
AX = mybir.AxisListType

P = 128
IMAGES, CH, ROWS, W = 8, 64, 64, 64
HR = ROWS // 2
COLS = HR * W
CHUNKS = 4
CW = COLS // CHUNKS
TPC = HR // CHUNKS
CR, TAPS = 16, 9
PR, PW = 4, 16
PK = (PR + 2) * (PW + 2)
RG, WP = HR // PR, W // PW
HEADS, DH, KR = 8, 32, 4
HKR = HEADS * KR
FF = 4 * W
HID = 128
EXPERTS, LAYERS = 16, 2
SEGS = 8
SEGC = CH // SEGS
EPS = 1e-5
EW = LAYERS * HID + LAYERS
WE_RING = 4

Y_HI_ROWS, Y_LO_ROW, Y_ONE_ROW, Y_ROWS = 96, 64, 96, 99
B_CONV, B_QK, B_ATT, B_MLP, B_FFN, B_ALL = 0, 96, 160, 224, 288, 352

SQUEEZE_LOADS, TAP_LOADS, WEIGHT_LOADS, PREP_DVE, PREP_MM = 7, 7, 20, 6, 4
EXPERT_TURNS = {6: 5, 7: 4}
HT = HR // 2
LN_STEPS = {0: 11, 2: 7, 3: 7}
Q_STEPS, K_STEPS = 5, 5

CONSTANTS = (("ident", P), ("bandmask", W), ("headcols", 2 * P), ("headrows", 4), ("ypick", 6), ("halfpick", 2))
GROUPS = 6
GROUP_HALF = (0, 0, 1, 1, 0, 1)

LAG = {"A": 0, "B": 1, "M": 2, "C": 3}

Image = namedtuple("Image", "i h p")


def after(eng, sem, value):
    if not isinstance(value, int) or value > 0:
        eng.wait_ge(sem, value)


class Banks:

    def __init__(self, banks, uses, filled, freed, earlier={}):
        self.place = {}
        self.earlier = {b: earlier.get(b, 0) for b in banks}
        count = {b: 0 for b in banks}
        for n, use in enumerate(uses):
            b = banks[n % len(banks)]
            self.place[use] = (b, count[b])
            count[b] += 1
        self.count, self.filled, self.freed = count, filled, freed

    def claim(self, pe, im, *use, needs=()):
        b, k = self.place[use]
        least = {b: k}
        for n in needs:
            c, m = self.place[n]
            least[c] = max(least.get(c, 0), m + 1)
        for c, m in least.items():
            after(pe, self.freed[c], im.i * self.count[c] + (self.earlier[c] + m))
        return b

    def full(self, eng, im, *use):
        b, k = self.place[use]
        after(eng, self.filled[b], im.i * self.count[b] + (self.earlier[b] + k + 1))
        return b

    def taken(self, eng, im, *use):
        b, k = self.place[use]
        after(eng, self.freed[b], im.i * self.count[b] + (self.earlier[b] + k + 1))


SLOT_ORDER = """
    A conv 0, M ft 0, M ft 1, B scale 0, B z 0, A regroup 0, C z3t 0, C z3t 1, A conv 1, M w1 0 0, M w1 0 1,
    M low 0, A regroup 1, B zt 0, A conv 2, M w1 0 2, C z3t 2, A conv 3, C z3t 3, B zt 1, A regroup 2, M w1 0 3,
    M w1 1 0, A filters 0 0, B scale 1, M w2 0 0, B logits 0, A filters 1 0, A filters 0 1, B zt 2,
    A filters 1 1, M w1 1 1, A filters 0 2, M low 1, B logits 1, A filters 1 2, A filters 0 3, M w2 0 1,
    M low 2, M w1 1 2, M w2 0 2, B zt 3, A filters 1 3, A patches 0, M w1 1 3, M w2 0 3, M ft 2, M stats3 0,
    B logits 2, A regroup 3, A regroup 4, A patches 1, A patches 2, M w1 2 0, B logits 3, A patches 3, B z 1,
    M w2 1 0, A regroup 5, M low 3, M w1 2 1, A regroup 6, A involve 0, C ffn 0, B kmax, M w2 1 1, M w1 2 2,
    M w2 1 2, M w1 2 3, M low 4, M w2 1 3, M ft 3, A patches 4, M stats3 1, A regroup 7, A patches 5,
    A involve 1, A patches 6, B kshift, A patches 7, A stats0 0, M w1 3 0, A stats0 1, A prepare, M w2 2 0,
    C ffn 1, B pool, M w1 3 1, M w2 2 1, B mix, M low 5, M w1 3 2, B mixt, M w2 2 2, M low 6, M w1 3 3,
    M w2 2 3, M low 7, M norm3 0, A involve 2, A load, A norm0 0, B qt 0, M w2 3 0, M stats3 2, M w2 3 1,
    B qt 1, M w2 3 2, M w2 3 3, M stats3 3, M split3 0, M norm3 1, A involve 3, C ffn 2, A stats0 2, B attend 0,
    B stats2 0, B attend 1, C hlow 0, C ffn 3, C hlow 1, C ffn 4, B stats2 1, B fx 0, B attend 2, C hlow 2,
    C ffn 5, B stats2 2, A stats0 3, B attend 3, C hlow 3, C ffn 6, C hlow 4, B stats2 3, C ffn 7, C hlow 5,
    C ffn 8, C ffn 9, C hlow 6, C hlow 7, B norm2 0, C out 0, C out 1, B experts, M split3 1, B fx 1, B norm2 1,
    B split2 0, A norm0 1, C out 2, C out 3, B split2 1
"""


def slot_order():
    steps = [entry.split() for entry in SLOT_ORDER.split(",")]
    return [(name, stage, *map(int, args)) for stage, name, *args in steps]


def tower_kernel(nc, A, out):
    ctx = ExitStack()
    with ctx:
        def sb(name, shape, dt=F32):
            return ctx.enter_context(nc.sbuf_tensor(name, shape, dt))

        def sem(name):
            return ctx.enter_context(nc.semaphore(name))

        consts = sb("consts", [P, sum(w for _, w in CONSTANTS)])
        at = {}
        for name, w in CONSTANTS:
            at[name] = consts[:, sum(at[n].shape[1] for n in at):][:, 0:w]
        ident, bandmask, headrows = at["ident"], at["bandmask"][0:PK, :], at["headrows"]
        headcols = at["headcols"].rearrange("p (b n) -> p b n", b=2)
        ypick = at["ypick"][0:Y_ROWS, :].rearrange("p (h k) -> p h k", h=2)
        halfpick = at["halfpick"][0:Y_HI_ROWS, :]
        ident16 = sb("ident16", [P, P], F16)
        ones_col = sb("ones_col", [P, 1])
        ones3 = sb("ones3", [3, CW], BF16)
        neg_half = sb("neg_half", [P, HR])
        factor = sb("factor", [P, 4, HR])
        HALF, QUARTER, PER_W, EPSILON = range(4)

        conv_w = sb("conv_w", [P, Y_HI_ROWS])
        tap_w = sb("tap_w", [Y_ROWS, 2, PR, 3, PR + 2, PW + 2], F16)
        qk_w = sb("qk_w", [P, 2 * 2 * HKR])
        head_w = sb("head_w", [P, HEADS, W])
        head_b = sb("head_b", [P, W])
        w1_hh = sb("w1_hh", [P, FF], F16)
        w1_l0 = sb("w1_l0", [P, FF], F16)
        b1_col = sb("b1_col", [P, 2])
        w2_hi = sb("w2_hi", [P, 2, W], F16)
        w2_lo = sb("w2_lo", [P, 2, W], F16)
        wi_hh = sb("wi_hh", [P, HID], F16)
        wi_l0 = sb("wi_l0", [P, HID], F16)
        bi_col = sb("bi_col", [P, 1])
        fo_hi = sb("fo_hi", [P, W], F16)
        fo_lo = sb("fo_lo", [P, W], F16)
        bias_rows = sb("bias_rows", [3, B_ALL], BF16)

        xpad = sb("xpad", [P, HR + 2, W + 2])
        y16 = sb("y16", [Y_ROWS, COLS], F16)
        xrun = sb("xrun", [P, 4, WP, PR + 2, PW + 2])
        xpatch = sb("xpatch", [PK, 4, WP, P])
        wide = sb("wide", [P, 2, COLS])
        h0 = [sb(f"h0_{p}", [P, COLS]) for p in range(2)]
        zn = sb("zn", [P, COLS])
        z = sb("z", [P, COLS])
        zT = sb("zT", [P, 2, CW])
        lg = sb("lg", [P, HR, 2 * HKR])
        q = sb("q", [P, HR, HKR])
        qT = sb("qT", [P, 2 * CHUNKS, P])
        sp2 = sb("sp2", [P, HR, 2 * W], F16)
        sp3 = sb("sp3", [P, HR, 2 * W], F16)
        fT = sb("fT", [P, 2, TPC * P], F16)
        gelu = sb("gelu", [P, 2, 2, 512])
        ge_hi = sb("ge_hi", [P, 3, 2, 512], F16)
        ge_lo = sb("ge_lo", [P, 3, 2, 512], F16)
        h1 = [sb(f"h1_{p}", [P, COLS]) for p in range(2)]
        normed = sb("normed", [P, COLS])
        z3T = sb("z3T", [P, HR, 2, CH], F16)
        hid_a = sb("hid_a", [P, 2, 512])
        hid_b = sb("hid_b", [P, 2, 512])
        ew = sb("ew", [P, WE_RING, EW])
        route = sb("route", [1, IMAGES * SEGS], I32)
        filt = [wide[0:PK, hh, :] for hh in range(2)]
        hid_hi, hid_lo = [wide[:, k, :].bitcast(F16).rearrange("p (t hh c) -> p t hh c", hh=2, c=CH) for k in range(2)]

        bn = {k: sb(f"bn{k}", [P, HR, 6]) for k in (0, 2, 3)}
        st = {k: sb(f"st{k}", [P, 8, HR]) for k in (0, 2, 3)}
        kmx = sb("kmx", [P, HKR])
        kmb = sb("kmb", [HKR, P])
        kmc = sb("kmc", [HKR, 1])
        ksum = sb("ksum", [P, 4, HKR])
        qmx = sb("qmx", [P, HR, HEADS])
        qden = sb("qden", [P, HR, HEADS])
        qinv = sb("qinv", [P, HR, HEADS])
        khT = sb("khT", [P, HKR])
        kinv = sb("kinv", [P, 1])
        gT4 = sb("gT4", [P, 4, HKR])
        gmix = sb("gmix", [P, 4, W])
        psum = ctx.enter_context(nc.psum_tensor("psum", [P, 8, 512], F32))

        flat_a, flat_b = [v[:, :, :].rearrange("p a n -> p (a n)") for v in (hid_a, hid_b)]
        s_wx = h1[1][0:W, 0:256]
        s_wxT = h1[1][:, 256:512].rearrange("p (b d w) -> p b d w", b=2, d=2)
        s_bdqk = h1[1][:, 512:544]
        s_bdv = h1[1][:, 576:704]
        s_wo = h1[1][:, 704:832].rearrange("p (b c) -> p b c", b=2)
        s_wom = h1[1][:, 832:1344].rearrange("p (b h c) -> p b h c", b=2, h=4)
        s_w2 = flat_b[:, 0:P].rearrange("p (f c) -> p f c", f=2)
        s_w1 = h1[1][:, 1344:1600]
        s_w1g = h1[1][:, 1600:1856]
        s_vxT = h1[1][:, 1856:1984].rearrange("p (b w) -> p b w", b=2)
        s_wi = normed[:, 0:128].rearrange("p (d w) -> p d w", d=2)
        s_fo = normed[0:W, 128:256]
        s_cw = normed[0:Y_HI_ROWS, 256:384]
        s_cp = normed[0:Y_HI_ROWS, 384:392]
        s_cb3 = normed[0:Y_HI_ROWS, 392:395]
        s_cols = normed[:, 400:416]
        s_u3 = normed[:, 416:422].rearrange("p (b k) -> p b k", b=2)
        s_vbx = normed[:, 448:704].rearrange("p (b k) -> p b k", b=2)
        s_w2f = normed[0:Y_ROWS, 704:713]
        s_w2r = normed[0:Y_ROWS, 736:745]
        s_w2a = normed[0:Y_ROWS, 752:770].rearrange("p (h k) -> p h k", h=2)
        s_brf = normed[0:3, 912:912 + B_ALL]
        s_brr = normed[0:3, 1280:1280 + B_ALL]
        s_bra = normed[0:3, 1664:1664 + B_ALL]
        w2h16, w2m16, w2l16 = [zn[0:Y_ROWS, 128 + 8 * k:136 + 8 * k].bitcast(F16)[:, 0:TAPS] for k in range(3)]
        w2d16 = zn[0:Y_ROWS, 160:178].bitcast(F16).rearrange("p (h i j) -> p h i j", h=2, i=3)
        brh, brm, brl = [flat_a[0:3, 176 * k:176 * k + 176].bitcast(BF16) for k in range(3)]
        s_cwx = flat_b[0:Y_HI_ROWS, 512:576]
        s_cwp = flat_b[0:Y_HI_ROWS, 584:586]
        s_wq, s_wk, s_wv = flat_b[:, 576:580], flat_b[:, 580:584], flat_b[:, 592:624]
        e_nat = [v[:, :].rearrange("p (e k) -> p e k", e=EXPERTS) for v in h1]
        e_turn = [v[:, :, :].rearrange("p t w -> p (t w)").bitcast(F32).rearrange("p (e k) -> p e k", e=EXPERTS)
                  for v in (sp2, sp3)]
        e_ws = gelu[:, 0, 0, 0:LAYERS * HID].rearrange("p (l k) -> p l k", l=LAYERS)
        e_b = gelu[0:LAYERS * EXPERTS, 0, 1, 0:2 * HID].rearrange("p (a k) -> p a k", a=2)
        e_bT = sb("e_bT", [P, EXPERTS, LAYERS])
        expert_w = nc.dram_tensor("expert_w", [EXPERTS, P, EW], F32, kind="Internal").ap()

        zeroed = sem("zeroed")
        squeeze_in, taps_in, weights_in = sem("squeeze_in"), sem("taps_in"), sem("weights_in")
        prep_mm, prep_dve = sem("prep_mm"), sem("prep_dve")
        prep_link, var_eps, pow_done = sem("prep_link"), sem("var_eps"), sem("pow_done")
        experts_in, experts_sum, experts_out = sem("experts_in"), sem("experts_sum"), sem("experts_out")
        filled = [sem(f"filled{b}") for b in range(8)]
        freed = [sem(f"freed{b}") for b in range(8)]
        x_in, regrouped = sem("x_in"), sem("regrouped")
        y_hi = sem("y_hi")
        bn_done = {k: sem(f"bn_done{k}") for k in (0, 2, 3)}
        ln_step = {k: sem(f"ln_step{k}") for k in (0, 2, 3)}
        z_centred, z_ready, scale_ready, zn_ready = sem("z_centred"), sem("z_ready"), sem("scale_ready"), sem("zn_ready")
        q_step, k_step, q_exp, k_exp = sem("q_step"), sem("k_step"), sem("q_exp"), sem("k_exp")
        fx_added, n2_ready, hi2, lo2 = sem("fx_added"), sem("n2_ready"), sem("hi2"), sem("lo2")
        ge_high, ge_low = sem("ge_high"), sem("ge_low")
        n3_ready, hi3, lo3 = sem("n3_ready"), sem("hi3"), sem("lo3")
        hid_high, hid_low = sem("hid_high"), sem("hid_low")
        ew_in = [sem(f"ew_in{k}") for k in range(WE_RING)]
        h1_dma = [sem(f"h1_dma{p}") for p in range(2)]

        uses = {"A": [], "B": [], "M": [], "w2": [], "C": []}
        for name, stage, *args in slot_order():
            if name == "ffn":
                t, = args
                uses["C"] += [("wi", t)] * (t < SEGS) + [("e1", t - 1)] * (1 <= t <= SEGS) + [("e2", t - 2)] * (t >= 2)
            elif name == "w2":
                uses["w2"] += [("w2", args[0])] * (args[1] == 0)
            elif name in ("conv", "filters", "patches", "involve", "zt", "logits", "kmax", "kshift", "pool", "mix",
                          "mixt", "qt", "attend", "ft", "w1", "z3t", "out"):
                uses[stage].append((name, *args))
        bank_a = Banks([0, 1], uses["A"], filled, freed)
        bank_b = Banks([2], uses["B"], filled, freed)
        bank_m = Banks([3, 4], uses["M"], filled, freed)
        bank_w2 = Banks([5], uses["w2"], filled, freed)
        bank_c = Banks([6, 7], uses["C"], filled, freed, earlier=EXPERT_TURNS)

        def before(im, n=1):
            return Image(im.i - n, None, None)

        def run(steps, images):
            for name, stage, *args in slot_order():
                if name in steps and stage in images:
                    steps[name](images[stage], *args)

        def slots(eng, steps, first={}, second={}):
            def peeled(s):
                return {k: Image(s - n, (s - n) // 2, (s - n) % 2) for k, n in LAG.items() if 0 <= s - n < IMAGES}

            last = max(LAG.values())
            for s in range(last):
                run({**steps, **({0: first, 1: second}.get(s, {}))}, peeled(s))
            pairs = (IMAGES - last) // 2
            with eng.Fori(0, pairs) as j:
                for d in range(2):
                    run(steps, {k: Image(2 * j + (last + d - n), j + (last + d - n) // 2, (last + d - n) % 2)
                                for k, n in LAG.items()})
            for s in range(last + 2 * pairs, IMAGES + last):
                run(steps, peeled(s))

        def tiles(ap):
            return ap.rearrange("p (t w) -> p t w", w=W)

        def segment(ap):
            return ap.rearrange("p (t hh c) -> p t hh c", hh=2, c=SEGC)

        def chunk(ap, c):
            return ap[:, CW * c:CW * c + CW]

        block = ctx.enter_context(nc.Block())

        @block.sync
        def _(sp):
            def load(sem, dst, src, slow=False):
                n_in[sem] = n_in.get(sem, 0) + 1
                sp.dma_start(dst, src, allow_slow_non_contiguous=slow).then_inc(sem, 16)

            def rows(v, times=1):
                return bass.AP(v.tensor, v.offset, [[0, times], [1, v.shape[0]], [1, 1]])

            def load_x(im):
                x = A["x"][im.i]
                sp.dma_start(xpad[0:CH, 1:HR + 2, 1:W + 1], x[:, 0:HR + 1, :]).then_inc(x_in, 16)
                sp.dma_start(xpad[CH:P, 0:HR + 1, 1:W + 1], x[:, HR - 1:ROWS, :]).then_inc(x_in, 16)

            n_in = {}
            load(squeeze_in, s_cwx, A["L0_tok_conv1_w"].unsqueeze(0).to_broadcast([GROUPS, CR, CH]))
            for k, name in enumerate(("conv1_b", "bn_gamma", "bn_beta", "bn_mean", "bn_var")):
                load(squeeze_in, s_cp[:, k:k + 1], rows(A["L0_tok_" + name], GROUPS))
            load(squeeze_in, consts[:, :], A["constants"])
            taps = A["L0_tok_conv2_w"].rearrange("k o -> o k")
            sp.wait_ge(zeroed, 1)
            load_x(Image(0, 0, 0))
            for g in range(GROUPS):
                load(taps_in, s_w2f[CR * g:CR * g + CR, :], taps, slow=True)
            load(taps_in, s_w2f[Y_ONE_ROW:Y_ROWS, :], A["L0_tok_conv2_b"].unsqueeze(0).to_broadcast([3, TAPS]))
            load(weights_in, s_wx, A["L0_attn_Wx"])
            for v, name in ((s_wq, "Wq"), (s_wk, "Wk"), (s_wv, "Wv")):
                w = A["L0_attn_" + name]
                load(weights_in, v, w.unsqueeze(0).to_broadcast([4, DH, w.shape[1]]))
            load(weights_in, s_wo, A["L0_attn_Wo"].rearrange("(b p) c -> p b c", p=P))
            load(weights_in, s_w1, A["L0_attn_W1"].unsqueeze(0).to_broadcast([2, W, FF]))
            load(weights_in, s_wi, A["L0_ffn_Wi"].unsqueeze(1).to_broadcast([P, 2, W]))
            for k, name in ((0, "ln1_g"), (4, "ln2_g"), (1, "ln1_b"), (5, "ln2_b")):
                load(weights_in, s_cols[:, k:k + 1], rows(A["L0_attn_" + name], 2))
            for k, name in ((2, "bx"), (6, "b1")):
                load(weights_in, s_cols[:, k:k + 2], A["L0_attn_" + name].rearrange("(b p) -> p b", p=P), slow=True)
            for a, name in ((B_ATT, "L0_attn_bo"), (B_MLP, "L0_attn_b2"), (B_FFN, "L0_ffn_bo")):
                load(weights_in, s_brf[:, a:a + W], A[name].unsqueeze(0).to_broadcast([3, W]))
            load(weights_in, s_w2, A["L0_attn_W2"].rearrange("(f p) c -> p f c", p=P))
            load(weights_in, s_fo, A["L0_ffn_Wo"])
            load(weights_in, bi_col[:, :], rows(A["L0_ffn_bi"]))
            load(weights_in, route[:, :], A["L0_ffn_route_id"].unsqueeze(0))
            assert n_in == {squeeze_in: SQUEEZE_LOADS, taps_in: TAP_LOADS, weights_in: WEIGHT_LOADS}, n_in

            for l in range(LAYERS):
                if l == 1:
                    sp.wait_ge(prep_dve, PREP_DVE)
                    sp.wait_ge(prep_mm, PREP_MM)
                sp.dma_start(e_nat[l], A["L0_ffn_Wr"][l].rearrange("e o k -> o e k")).then_inc(h1_dma[l], 16)
                sp.dma_start(e_ws[:, l, :], A["L0_ffn_Ws"][l, 0]).then_inc(experts_in, 16)
                sp.dma_start(e_b[EXPERTS * l:EXPERTS * l + EXPERTS, 0, :], A["L0_ffn_br"][l]).then_inc(experts_in, 16)
                sp.dma_start(e_b[EXPERTS * l:EXPERTS * l + EXPERTS, 1, :],
                             A["L0_ffn_bs"][l].to_broadcast([EXPERTS, HID])).then_inc(experts_in, 16)

            def experts(im):
                ewd = expert_w.rearrange("e p k -> p e k")
                for b, n in EXPERT_TURNS.items():
                    sp.wait_ge(freed[b], n)
                for l in range(LAYERS):
                    sp.dma_start(ewd[:, :, l * HID:(l + 1) * HID], e_turn[l]).then_inc(experts_out, 16)
                sp.dma_start(ewd[:, :, LAYERS * HID:EW], e_bT[:, :, :]).then_inc(experts_out, 16)

            def load_next(im):
                if isinstance(im.i, int) and im.i == IMAGES - 1:
                    return
                bank_a.full(sp, im, "conv", CHUNKS - 1)
                sp.wait_ge(regrouped, RG * im.i + RG)
                load_x(before(im, -1))

            def fetch(im, s):
                if s >= WE_RING:
                    bank_c.taken(sp, im, "e2", s - WE_RING)
                n = SEGS * im.i + s
                e = sp.value_load(route[0:1, bass.ds(n, 1)], min_val=0, max_val=EXPERTS - 1)
                sp.dma_start(ew[:, s % WE_RING, :], expert_w[e]).then_inc(ew_in[s % WE_RING], 16)

            def ffn(im, t):
                if t == 0:
                    if isinstance(im.i, int) and im.i == 0:
                        sp.wait_ge(experts_out, 48)
                        sp.wait_ge(weights_in, 16 * WEIGHT_LOADS)
                    for s in range(WE_RING):
                        fetch(im, s)
                elif 3 <= t <= SEGS - 2:
                    fetch(im, t + 1)

            def store(im, c):
                bank_c.taken(sp, im, "out", c)
                o = out[im.i].rearrange("(c hh t) w -> hh c (t w)", hh=2, t=HR)
                for hh in range(2):
                    sp.dma_start(o[hh, :, CW * c:CW * c + CW],
                                 h1[im.p][CH * hh:CH * hh + CH, CW * c:CW * c + CW]).then_inc(h1_dma[im.p], 16)

            slots(sp, {"load": load_next, "ffn": ffn, "out": store},
                  second={"experts": experts})
            for p in range(2):
                sp.wait_ge(h1_dma[p], 16 + 16 * 2 * CHUNKS * (IMAGES // 2))

        @block.gpsimd
        def _(pool):
            for k, v in ((HALF, 0.5), (QUARTER, 0.25), (PER_W, 1.0 / W), (EPSILON, EPS)):
                pool.memset(factor[:, k, :], v)
            pool.memset(neg_half[:, :], -0.5).then_inc(pow_done, 1)
            pool.wait_ge(pow_done, 1)
            pool.wait_ge(var_eps, 1)
            pool.tensor_tensor(s_cp[:, 6:7], s_cp[:, 5:6], neg_half[0:Y_HI_ROWS, 0:1], ALU.pow).then_inc(pow_done, 1)

            link_count = {}
            c_eps = factor[:, EPSILON, 0:HT]

            def statistics(kind, im, g):
                t = slice(HT * g, HT * g + HT)
                s, c = st[kind][:, :, t], factor[:, :, 0:HT]
                me, mo, ve, vo = (bn[kind][:, t, k] for k in (1, 4, 2, 5))
                count = [g * LN_STEPS[kind]]

                def link(ins):
                    count[0] += 1
                    link_count[kind] = count[0]
                    ins.then_inc(ln_step[kind], 1)
                    pool.wait_ge(ln_step[kind], 2 * LN_STEPS[kind] * im.i + count[0])

                pool.wait_ge(bn_done[kind], CHUNKS * im.i + (2 * g + 2))
                pool.tensor_tensor(s[:, 1, :], me, mo, ALU.add)
                pool.tensor_tensor(s[:, 2, :], me, mo, ALU.subtract)
                link(pool.tensor_tensor(s[:, 3, :], ve, vo, ALU.add))
                pool.tensor_tensor(s[:, 0, :], s[:, 1, :], c[:, HALF, :], ALU.mult)
                pool.tensor_tensor(s[:, 3, :], s[:, 3, :], c[:, PER_W, :], ALU.mult)
                link(pool.tensor_tensor(s[:, 4, :], s[:, 2, :], s[:, 2, :], ALU.mult))
                link(pool.tensor_tensor(s[:, 4, :], s[:, 4, :], c[:, QUARTER, :], ALU.mult))
                link(pool.tensor_tensor(s[:, 5, :], s[:, 3, :], s[:, 4, :], ALU.add))
                link(pool.tensor_tensor(s[:, 6, :], s[:, 5, :], c[:, EPSILON, :], ALU.add))
                link(pool.tensor_tensor(s[:, 7, :], s[:, 6, :], neg_half[:, 0:HT], ALU.pow))
                return link, s

            def half(ap, g):
                return tiles(ap)[:, HT * g:HT * g + HT, :]

            def spread(s, k):
                return s[:, k, :].unsqueeze(2).to_broadcast([P, HT, W])

            def norm0(im, g):
                after(pool, zn_ready, 2 * (im.i - 1) + (g + 1))
                link, s = statistics(0, im, g)
                bank_b.full(pool, before(im), "pool")
                link(pool.tensor_tensor(half(zn[:, :], g), half(h0[im.p][:, :], g), spread(s, 0), ALU.subtract))
                link(pool.tensor_tensor(s[:, 4, :], s[:, 7, :], s[:, 7, :], ALU.mult))
                link(pool.tensor_tensor(s[:, 4, :], s[:, 4, :], s[:, 5, :], ALU.mult))
                link(pool.tensor_tensor(s[:, 4, :], s[:, 4, :], c_eps, ALU.add))
                link(pool.tensor_tensor(s[:, 6, :], s[:, 4, :], neg_half[:, 0:HT], ALU.pow))
                pool.tensor_tensor(s[:, 1, :], s[:, 6, :], s[:, 7, :], ALU.mult).then_inc(scale_ready, 1)
                assert link_count[0] == (g + 1) * LN_STEPS[0]

            def first_norm(im, g):
                s = st[0][:, :, HT * g:HT * g + HT]
                after(pool, lo2, 2 * (im.i - 1) + (g + 1))
                pool.tensor_tensor(half(z[:, :], g), half(h0[im.p][:, :], g), spread(s, 0),
                                   ALU.subtract).then_inc(z_centred, 1)
                pool.wait_ge(z_centred, 2 * im.i + (g + 1))
                pool.tensor_tensor(half(z[:, :], g), half(z[:, :], g), spread(s, 7), ALU.mult).then_inc(z_ready, 1)

            def fx(im, g):
                pool.wait_ge(bn_done[2], CHUNKS * im.i + (2 * g + 2))
                pool.tensor_tensor(half(h0[im.p][:, :], g), half(h0[im.p][:, :], g), half(z[:, :], g),
                                   ALU.add).then_inc(fx_added, 1)

            def norm2(im, g):
                link, s = statistics(2, im, g)
                pool.wait_ge(fx_added, 2 * im.i + (g + 1))
                link(pool.tensor_tensor(half(z[:, :], g), half(z[:, :], g), spread(s, 0), ALU.subtract))
                pool.tensor_tensor(half(z[:, :], g), half(z[:, :], g), spread(s, 7), ALU.mult).then_inc(n2_ready, 1)
                assert link_count[2] == (g + 1) * LN_STEPS[2]

            def norm3(im, g):
                link, s = statistics(3, im, g)
                after(pool, lo3, 2 * (im.i - 1) + (g + 1))
                link(pool.tensor_tensor(half(normed[:, :], g), half(h1[im.p][:, :], g), spread(s, 0), ALU.subtract))
                pool.tensor_tensor(half(normed[:, :], g), half(normed[:, :], g), spread(s, 7),
                                   ALU.mult).then_inc(n3_ready, 1)
                assert link_count[3] == (g + 1) * LN_STEPS[3]

            slots(pool, {"norm0": norm0, "z": first_norm, "norm2": norm2, "fx": fx, "norm3": norm3})

        @block.scalar
        def _(act):
            def conv(im, c):
                b = bank_a.full(act, im, "conv", c)
                act.activation(chunk(y16, c)[0:Y_HI_ROWS], psum[0:Y_HI_ROWS, b, :], ACT.Relu).then_inc(y_hi, 1)

            def patches(im, g):
                b = bank_a.full(act, im, "patches", g)
                act.activation(xpatch[:, g % 4, :, :], psum[0:PK, b, :].rearrange("p (a n) -> p a n", a=WP),
                               ACT.Copy).then_inc(freed[b], 1)

            def involve(im, c):
                b = bank_a.full(act, im, "involve", c)
                bank_w2.taken(act, before(im, 2), "w2", c)
                act.activation(chunk(h0[im.p], c), psum[:, b, :], ACT.Copy).then_inc(freed[b], 1)

            def zt(im, c):
                b = bank_b.full(act, im, "zt", c)
                act.activation(zT[:, c % 2, :], psum[:, b, :], ACT.Copy).then_inc(freed[b], 1)

            def logits(im, c):
                b = bank_b.full(act, im, "logits", c)
                act.activation(lg[:, TPC * c:TPC * c + TPC, :], psum[:, b, :].rearrange("p (t k) -> p t k", t=TPC),
                               ACT.Copy).then_inc(freed[b], 1)

            def kshift(im):
                act.wait_ge(q_step, Q_STEPS * im.i + 2)
                act.activation(lg[:, :, 0:HKR], lg[:, :, 0:HKR], ACT.Exp).then_inc(q_exp, 1)
                bank_b.taken(act, im, "kshift")
                act.activation(lg[:, :, HKR:2 * HKR], lg[:, :, HKR:2 * HKR], ACT.Exp).then_inc(k_exp, 1)

            def qt(im, j):
                b = bank_b.full(act, im, "qt", j)
                act.activation(qT[:, 4 * j:4 * j + 4, :], psum[:, b, :].rearrange("p (k n) -> p k n", k=4),
                               ACT.Copy).then_inc(freed[b], 1)

            def split2(im, g):
                if isinstance(im.i, int) and im.i == 0:
                    act.wait_ge(experts_out, 48)
                act.wait_ge(n2_ready, 2 * im.i + (g + 1))
                bank_m.full(act, before(im), "ft", 2 * g + 1)
                act.activation(sp2[:, 16 * g:16 * g + 16, 0:W], tiles(z[:, :])[:, 16 * g:16 * g + 16, :],
                               ACT.Copy).then_inc(hi2, 1)

            def split3(im, g):
                act.wait_ge(n3_ready, 2 * im.i + (g + 1))
                bank_c.full(act, before(im), "z3t", 2 * g + 1)
                act.activation(sp3[:, 16 * g:16 * g + 16, 0:W], tiles(normed[:, :])[:, 16 * g:16 * g + 16, :],
                               ACT.Copy).then_inc(hi3, 1)

            def w1(im, c, k):
                u, f = 2 * c + k // 2, k % 2
                b = bank_m.full(act, im, "w1", c, k)
                if f == 0:
                    after(act, ge_low, 2 * CHUNKS * im.i + u - 1)
                act.activation(gelu[:, u % 2, f, :], psum[:, b, :], ACT.Gelu,
                               bias=b1_col[:, f:f + 1]).then_inc(freed[b], 1)
                if f == 1:
                    bank_m.taken(act, im, "w1", c, k - 1)
                    bank_m.taken(act, im, "w1", c, k)
                    act.activation(ge_hi[:, u % 3, :, :], gelu[:, u % 2, :, :], ACT.Copy).then_inc(ge_high, 1)

            def ffn(im, t):
                if t < SEGS:
                    b = bank_c.full(act, im, "wi", t)
                    act.activation(hid_a[:, t % 2, :], psum[:, b, :], ACT.Relu, bias=bi_col[:, :]).then_inc(freed[b], 1)
                if 1 <= t <= SEGS:
                    s = t - 1
                    b = bank_c.full(act, im, "e1", s)
                    if s >= 2:
                        act.wait_ge(hid_low, SEGS * im.i + s - 1)
                    act.activation(hid_b[:, s % 2, :], psum[:, b, :], ACT.Relu,
                                   bias=ew[:, s % WE_RING, LAYERS * HID:LAYERS * HID + 1]).then_inc(freed[b], 1)
                if t >= 2:
                    s = t - 2
                    b = bank_c.full(act, im, "e2", s)
                    act.activation(hid_b[:, s % 2, :], psum[:, b, :], ACT.Relu,
                                   bias=ew[:, s % WE_RING, LAYERS * HID + 1:LAYERS * HID + 2]).then_inc(freed[b], 1)
                    bank_c.taken(act, im, "e2", s)
                    act.activation(hid_hi[:, :, :, SEGC * s:SEGC * s + SEGC], segment(hid_b[:, s % 2, :]),
                                   ACT.Copy).then_inc(hid_high, 1)

            def prepare(im):
                act.wait_ge(prep_dve, PREP_DVE)

            slots(act, {"conv": conv, "patches": patches, "involve": involve, "zt": zt, "logits": logits,
                        "kshift": kshift, "qt": qt, "split2": split2, "split3": split3, "w1": w1, "ffn": ffn},
                  first={"prepare": prepare})

        @block.vector
        def _(dve):
            chain = [0]

            def link(ins):
                chain[0] += 1
                ins.then_inc(prep_link, 1)
                dve.wait_ge(prep_link, chain[0])

            def done(ins):
                ins.then_inc(prep_dve, 1)

            dve.memset(xpad[:, :, :], 0.0).then_inc(zeroed, 1)
            dve.memset(y16[Y_ONE_ROW:Y_ROWS, :], 1.0)
            dve.memset(ones3[:, :], 1.0)
            link(dve.memset(tap_w[:, :, :, :, :, :], 0.0))

            dve.wait_ge(squeeze_in, 16 * SQUEEZE_LOADS)
            dve.tensor_scalar(s_cp[:, 5:6], s_cp[:, 4:5], EPS, None, ALU.add).then_inc(var_eps, 1)
            dve.wait_ge(pow_done, 2)
            link(dve.tensor_tensor(s_cp[:, 7:8], s_cp[:, 6:7], s_cp[:, 1:2], ALU.mult))
            link(dve.tensor_tensor(s_cp[:, 5:6], s_cp[:, 0:1], s_cp[:, 3:4], ALU.subtract))
            link(dve.tensor_tensor(s_cp[:, 5:6], s_cp[:, 5:6], s_cp[:, 7:8], ALU.mult))
            dve.tensor_scalar(s_cwp, halfpick, s_cp[:, 7:8], None, ALU.mult)
            link(dve.tensor_tensor(s_cp[:, 5:6], s_cp[:, 5:6], s_cp[:, 2:3], ALU.add))
            for hh in range(2):
                dve.tensor_scalar(s_cw[:, CH * hh:CH * hh + CH], s_cwx, s_cwp[:, hh:hh + 1], None, ALU.mult)
            done(dve.tensor_copy(s_cb3, s_cp[:, 5:6].to_broadcast([Y_HI_ROWS, 3])))

            def bias_parts(a, n):
                c = slice(a, a + n)
                link(dve.tensor_copy(brh[:, c], s_brf[:, c]))
                link(dve.tensor_tensor(s_brr[:, c], s_brf[:, c], brh[:, c], ALU.subtract))
                link(dve.tensor_copy(brm[:, c], s_brr[:, c]))
                link(dve.tensor_tensor(brl[:, c], s_brr[:, c], brm[:, c], ALU.subtract))
                link(dve.tensor_scalar(s_bra[:, c], brh[:, c], ident[0:3, 0:1], None, ALU.mult))
                link(dve.scalar_tensor_tensor(s_bra[:, c], brm[:, c], ident[0:3, 1:2], s_bra[:, c], ALU.mult, ALU.add))
                return dve.scalar_tensor_tensor(bias_rows[:, c], brl[:, c], ident[0:3, 2:3], s_bra[:, c],
                                                ALU.mult, ALU.add)

            dve.wait_ge(prep_mm, 1)
            dve.tensor_copy(conv_w[:, :], psum[:, 4, 0:Y_HI_ROWS])
            link(dve.tensor_copy(s_brf[:, B_CONV:B_CONV + Y_HI_ROWS], psum[0:3, 5, 0:Y_HI_ROWS]))
            done(bias_parts(B_CONV, Y_HI_ROWS))

            dve.wait_ge(taps_in, 16 * TAP_LOADS)
            dve.tensor_copy(ident16[:, :], ident)
            link(dve.tensor_copy(w2h16, s_w2f))
            link(dve.tensor_tensor(s_w2r, s_w2f, w2h16, ALU.subtract))
            link(dve.tensor_copy(w2m16, s_w2r))
            link(dve.tensor_tensor(w2l16, s_w2r, w2m16, ALU.subtract))
            for hh in range(2):
                link(dve.tensor_scalar(s_w2a[:, hh, :], w2h16, ypick[:, hh, 0:1], None, ALU.mult))
                link(dve.scalar_tensor_tensor(s_w2a[:, hh, :], w2m16, ypick[:, hh, 1:2], s_w2a[:, hh, :],
                                              ALU.mult, ALU.add))
                link(dve.scalar_tensor_tensor(s_w2a[:, hh, :], w2l16, ypick[:, hh, 2:3], s_w2a[:, hh, :],
                                              ALU.mult, ALU.add))
                link(dve.tensor_copy(w2d16[:, hh, :, :].rearrange("p i (d j) -> p i d j", d=2),
                                     s_w2a[:, hh, :].rearrange("p (i j) -> p i j", i=3).unsqueeze(2)
                                     .to_broadcast([Y_ROWS, 3, 2, 3])))
                for r in range(PR):
                    for k in range(3):
                        a = (3 - k) % 3
                        last = dve.tensor_copy(tap_w[:, hh, r, k, r:r + 3, :].rearrange("p i (n j) -> p i n j", j=3),
                                               w2d16[:, hh, :, a:a + 3].unsqueeze(2).to_broadcast([Y_ROWS, 3, 6, 3]))
            done(last)

            def prepare(im):
                dve.memset(ones_col[:, :], 1.0)
                dve.memset(w1_l0[:, :], 0.0)
                dve.memset(wi_l0[:, :], 0.0)
                dve.memset(qk_w[:, :], 0.0)
                dve.memset(gmix[:, :, :], 0.0)
                for v in (head_w[:, :, :], khT[:, :], gT4[:, :, :]):
                    last = dve.memset(v, 0.0)
                link(last)
                dve.wait_ge(weights_in, 16 * WEIGHT_LOADS)
                by_head = headrows[:, :].unsqueeze(2)
                for v, w, n in ((s_bdqk[:, 0:16], s_wq, KR), (s_bdqk[:, 16:32], s_wk, KR), (s_bdv, s_wv, DH)):
                    dve.tensor_tensor(v.rearrange("p (h k) -> p h k", h=4), w.unsqueeze(1).to_broadcast([P, 4, n]),
                                      by_head.to_broadcast([P, 4, n]), ALU.mult)
                dve.wait_ge(prep_mm, 2)
                dve.tensor_copy(s_wxT, psum[:, 3, 0:2 * W].rearrange("p (b w) -> p b w", b=2).unsqueeze(2)
                                .to_broadcast([P, 2, 2, W]))
                link(dve.tensor_tensor(s_cols[:, 8:10], psum[:, 4, 0:2], s_cols[:, 2:4], ALU.add))
                dve.tensor_copy(s_u3, s_cols[:, 8:10].unsqueeze(2).to_broadcast([P, 2, 3]))
                dve.tensor_tensor(b1_col[:, :], psum[:, 4, 2:4], s_cols[:, 6:8], ALU.add)
                link(dve.tensor_copy(fo_hi[:, :], psum[:, 6, 0:W]))
                dve.tensor_tensor(fo_lo[:, :], psum[:, 6, 0:W], fo_hi[:, :], ALU.subtract)
                dve.tensor_scalar(s_w1g, s_w1, s_cols[:, 4:5], None, ALU.mult)
                link(dve.tensor_copy(wi_hh[:, :], psum[:, 5, 0:HID]))
                dve.tensor_tensor(wi_l0[0:W, :], psum[0:W, 5, 0:HID], wi_hh[0:W, :], ALU.subtract)
                link(dve.tensor_copy(w1_hh[:, :], s_w1g))
                link(dve.tensor_copy(w2_hi[:, :, :], s_w2))
                dve.tensor_tensor(w2_lo[:, :, :], s_w2, w2_hi[:, :, :], ALU.subtract)
                done(dve.tensor_tensor(w1_l0[0:W, :], s_w1g[0:W, :], w1_hh[0:W, :], ALU.subtract))

                dve.wait_ge(prep_mm, 3)
                for b in range(2):
                    dve.tensor_copy(s_brf[:, B_QK:B_QK + 2 * HKR].rearrange("p (a b n) -> p a b n", a=2, b=2)[:, :, b, :],
                                    psum[0:3, 7, 32 * b:32 * b + 32].rearrange("p (a n) -> p a n", a=2))
                    for d in range(2):
                        rows = slice(W * d, W * d + W)
                        dve.tensor_scalar(
                            qk_w[rows, 64 * d:64 * d + 64].rearrange("p (a b n) -> p a b n", a=2, b=2)[:, :, b, :],
                            psum[rows, 6, 128 + 32 * b:160 + 32 * b].rearrange("p (a n) -> p a n", a=2),
                            s_cols[rows, 0:1], None, ALU.mult)
                dve.tensor_copy(s_vxT, psum[:, 3, 0:2 * W].rearrange("p (b w) -> p b w", b=2))
                link(dve.tensor_copy(s_cols[:, 10:12], psum[:, 4, 0:2]))
                for b in range(2):
                    dve.tensor_scalar(s_vbx[:, b, :], headcols[:, b, :], s_cols[:, 10 + b:11 + b], None, ALU.mult)
                    ins = dve.tensor_tensor(s_wom[:, b, :, :], s_wo[:, b, :].unsqueeze(1).to_broadcast([P, 4, W]),
                                            headrows[:, :].unsqueeze(2).to_broadcast([P, 4, W]), ALU.mult)
                done(ins)
                link(bias_parts(B_QK, B_ALL - B_QK))

                dve.wait_ge(prep_mm, 4)
                for b in range(2):
                    dve.tensor_scalar(head_w[0:W, 4 * b:4 * b + 4, :],
                                      psum[0:W, 5 + b, 0:4 * W].rearrange("p (h c) -> p h c", h=4),
                                      s_cols[0:W, 0:1], None, ALU.mult)
                done(dve.tensor_copy(head_b[:, :], psum[:, 7, 64:64 + W]))

            def experts(im):
                dve.wait_ge(experts_in, 16 * 3 * LAYERS)
                for l in range(LAYERS):
                    dve.wait_ge(h1_dma[l], 16)
                    link(dve.tensor_tensor(e_ws[:, l, :], e_ws[:, l, :], ident[:, :], ALU.add))
                    v = e_nat[l]
                    dve.tensor_tensor(v, v, e_ws[:, l, :].unsqueeze(1).to_broadcast([P, EXPERTS, HID]),
                                      ALU.add).then_inc(experts_sum, 1)
                dve.tensor_tensor(e_b[:, 0, :], e_b[:, 0, :], e_b[:, 1, :], ALU.add).then_inc(experts_sum, 1)
                for n in range(8):
                    dve.wait_ge(filled[6 + n % 2], n // 2 + 1)
                    dve.tensor_copy(e_turn[n // 4][:, 4 * (n % 4):4 * (n % 4) + 4, :],
                                    psum[:, 6 + n % 2, :].rearrange("p (e k) -> p e k", e=4)
                                    ).then_inc(freed[6 + n % 2], 1)
                dve.wait_ge(filled[6], EXPERT_TURNS[6])
                dve.tensor_copy(e_bT[:, :, :].rearrange("p e l -> p l e"),
                                psum[:, 6, 0:LAYERS * EXPERTS].rearrange("p (l e) -> p l e", l=LAYERS)
                                ).then_inc(freed[6], 1)

            def conv(im, c):
                dve.wait_ge(y_hi, CHUNKS * im.i + (c + 1))
                b = bank_a.full(dve, im, "conv", c)
                lo = chunk(y16, c)[Y_LO_ROW:Y_HI_ROWS]
                dve.scalar_tensor_tensor(lo, psum[Y_LO_ROW:Y_HI_ROWS, b, :], 0.0, lo, ALU.max,
                                         ALU.subtract).then_inc(freed[b], 1)

            def regroup(im, g):
                if g == 0:
                    dve.wait_ge(x_in, 32 * im.i + 32)
                if g >= 4:
                    bank_a.full(dve, im, "patches", g - 4)
                else:
                    bank_a.full(dve, before(im), "patches", g + 4)
                rows = xpad[:, PR * g:PR * g + PR + 2, :]
                src = bass.AP(rows.tensor, rows.offset, [rows.ap[0], [PW, WP], rows.ap[1], [1, PW + 2]])
                dve.tensor_copy(xrun[:, g % 4, :, :, :], src).then_inc(regrouped, 1)

            def filters(im, hh, r):
                b = bank_a.full(dve, im, "filters", hh, r)
                dve.tensor_tensor(filt[hh].rearrange("p (g r w) -> p g r w", r=PR, w=W)[:, :, r, :],
                                  psum[0:PK, b, :].rearrange("p (g w) -> p g w", w=W),
                                  bandmask[:, :].unsqueeze(1).to_broadcast([PK, RG, W]), ALU.mult).then_inc(freed[b], 1)

            def stats(kind, ap, c):
                for t in range(TPC * c, TPC * c + TPC):
                    ins = dve.bn_stats(bn[kind][:, t, :], ap[:, W * t:W * t + W])
                ins.then_inc(bn_done[kind], 1)

            def stats0(im, c):
                bank_a.taken(dve, im, "involve", c)
                after(dve, scale_ready, 2 * (im.i - 1) + (c // 2 + 1))
                stats(0, h0[im.p], c)

            def scale(im, g):
                dve.wait_ge(scale_ready, 2 * im.i + (g + 1))
                v = tiles(zn[:, :])[:, 16 * g:16 * g + 16, :]
                dve.tensor_tensor(v, v, st[0][:, 1, 16 * g:16 * g + 16].unsqueeze(2).to_broadcast([P, 16, W]),
                                  ALU.mult).then_inc(zn_ready, 1)

            def kmax(im):
                bank_b.taken(dve, im, "logits", CHUNKS - 1)
                dve.tensor_reduce(kmx[:, :], lg[:, :, HKR:2 * HKR].rearrange("p t k -> p k t"), AX.X,
                                  ALU.max).then_inc(k_step, 1)
                ql = lg[:, :, 0:HKR].rearrange("p t (h r) -> p t h r", r=KR)
                dve.tensor_reduce(qmx[:, :, :], ql, AX.X, ALU.max).then_inc(q_step, 1)
                dve.wait_ge(q_step, Q_STEPS * im.i + 1)
                dve.tensor_tensor(ql, ql, qmx[:, :, :].unsqueeze(3).to_broadcast([P, HR, HEADS, KR]),
                                  ALU.subtract).then_inc(q_step, 1)

            def kshift(im):
                b = bank_b.full(dve, im, "kmax")
                dve.tensor_reduce(kmc[:, :], psum[0:HKR, b, 0:P], AX.X, ALU.max).then_inc(k_step, 1)
                dve.wait_ge(k_step, K_STEPS * im.i + 2)
                dve.tensor_copy(kmb[:, :], kmc[:, :].to_broadcast([HKR, P])).then_inc(freed[b], 1)
                b = bank_b.full(dve, im, "kshift")
                kl = lg[:, :, HKR:2 * HKR]
                dve.tensor_tensor(kl, kl, psum[:, b, 0:HKR].unsqueeze(1).to_broadcast([P, HR, HKR]),
                                  ALU.subtract).then_inc(freed[b], 1)

            def pool(im):
                ql = lg[:, :, 0:HKR].rearrange("p t (h r) -> p t h r", r=KR)
                dve.wait_ge(q_exp, im.i + 1)
                dve.tensor_reduce(qden[:, :, :], ql, AX.X, ALU.add).then_inc(q_step, 1)
                dve.wait_ge(q_step, Q_STEPS * im.i + 3)
                dve.reciprocal(qinv[:, :, :], qden[:, :, :]).then_inc(q_step, 1)
                dve.wait_ge(k_exp, im.i + 1)
                dve.tensor_reduce(kmx[:, :], lg[:, :, HKR:2 * HKR].rearrange("p t k -> p k t"), AX.X,
                                  ALU.add).then_inc(k_step, 1)
                dve.wait_ge(k_step, K_STEPS * im.i + 3)
                dve.tensor_copy(ksum[:, :, :], kmx[:, :].unsqueeze(1).to_broadcast([P, 4, HKR])).then_inc(k_step, 1)
                dve.wait_ge(q_step, Q_STEPS * im.i + 4)
                dve.tensor_tensor(q[:, :, :].rearrange("p t (h r) -> p t h r", r=KR), ql,
                                  qinv[:, :, :].unsqueeze(3).to_broadcast([P, HR, HEADS, KR]),
                                  ALU.mult).then_inc(q_step, 1)

            def mix(im):
                b = bank_b.full(dve, im, "pool")
                dve.reciprocal(kinv[:, :], psum[:, b, 64:65]).then_inc(k_step, 1)
                dve.tensor_copy(khT[0:W, :], psum[0:W, b, 0:HKR]).then_inc(freed[b], 1)

            def mixt(im):
                b = bank_b.full(dve, im, "mix")
                dve.tensor_copy(gT4[0:W, :, :], psum[0:W, b, 0:HKR].unsqueeze(1).to_broadcast([W, 4, HKR])
                                ).then_inc(freed[b], 1)
                b = bank_b.full(dve, im, "mixt")
                dve.wait_ge(k_step, K_STEPS * im.i + 5)
                for k in range(4):
                    rows = slice(HKR * k, HKR * k + HKR)
                    ins = dve.scalar_tensor_tensor(gmix[rows, k, :], psum[rows, b, 0:W], kinv[rows, :],
                                                   head_b[rows, :], ALU.mult, ALU.add)
                ins.then_inc(freed[b], 1)

            def attend(im, c):
                b = bank_b.full(dve, im, "attend", c)
                if c == 0:
                    dve.wait_ge(z_ready, 2 * im.i + 2)
                dve.tensor_tensor(chunk(z, c), psum[:, b, :], chunk(z, c), ALU.add).then_inc(freed[b], 1)

            def stats2(im, c):
                bank_b.taken(dve, im, "attend", c)
                after(dve, n2_ready, 2 * (im.i - 1) + (c // 2 + 1))
                stats(2, z, c)

            def split2(im, g):
                dve.wait_ge(hi2, 2 * im.i + (g + 1))
                t = slice(16 * g, 16 * g + 16)
                dve.tensor_tensor(sp2[:, t, W:2 * W], tiles(z[:, :])[:, t, :], sp2[:, t, 0:W],
                                  ALU.subtract).then_inc(lo2, 1)

            def split3(im, g):
                dve.wait_ge(hi3, 2 * im.i + (g + 1))
                t = slice(16 * g, 16 * g + 16)
                dve.tensor_tensor(sp3[:, t, W:2 * W], tiles(normed[:, :])[:, t, :], sp3[:, t, 0:W],
                                  ALU.subtract).then_inc(lo3, 1)

            def ft(im, c):
                b = bank_m.full(dve, im, "ft", c)
                dve.tensor_copy(fT[:, c % 2, :], psum[:, b, :].bitcast(F16)).then_inc(freed[b], 1)

            def z3t(im, c):
                b = bank_c.full(dve, im, "z3t", c)
                dve.tensor_copy(z3T[:, TPC * c:TPC * c + TPC, :, :].rearrange("p t hh c -> p (t hh c)"),
                                psum[:, b, :].bitcast(F16)).then_inc(freed[b], 1)

            def low(im, u):
                dve.wait_ge(ge_high, 2 * CHUNKS * im.i + (u + 1))
                dve.tensor_tensor(ge_lo[:, u % 3, :, :], gelu[:, u % 2, :, :], ge_hi[:, u % 3, :, :],
                                  ALU.subtract).then_inc(ge_low, 1)

            def w2(im, c, k):
                if k < 3:
                    return
                b = bank_w2.full(dve, im, "w2", c)
                if c == 0:
                    dve.wait_ge(fx_added, 2 * im.i + 2)
                    dve.wait_ge(h1_dma[im.p], 16 + 16 * 2 * CHUNKS * im.h)
                dve.tensor_tensor(chunk(h1[im.p], c), psum[:, b, :], chunk(h0[im.p], c), ALU.add).then_inc(freed[b], 1)

            def stats3(im, c):
                bank_w2.taken(dve, im, "w2", c)
                after(dve, n3_ready, 2 * (im.i - 1) + (c // 2 + 1))
                stats(3, h1[im.p], c)

            def hlow(im, s):
                dve.wait_ge(hid_high, SEGS * im.i + (s + 1))
                rows = slice(SEGC * s, SEGC * s + SEGC)
                dve.tensor_tensor(hid_lo[:, :, :, rows], segment(hid_b[:, s % 2, :]), hid_hi[:, :, :, rows],
                                  ALU.subtract).then_inc(hid_low, 1)

            def add_ffn(im, c):
                b = bank_c.full(dve, im, "out", c)
                v = chunk(h1[im.p], c)
                dve.tensor_tensor(v, psum[:, b, :], v, ALU.add).then_inc(freed[b], 1)

            slots(dve, {"conv": conv, "regroup": regroup, "filters": filters, "stats0": stats0, "scale": scale,
                        "kmax": kmax, "stats2": stats2, "stats3": stats3, "low": low, "hlow": hlow,
                        "kshift": kshift, "pool": pool, "mix": mix, "mixt": mixt, "attend": attend, "split2": split2,
                        "split3": split3, "ft": ft, "z3t": z3t, "w2": w2, "out": add_ffn},
                  first={"prepare": prepare}, second={"experts": experts})

        @block.tensor
        def _(pe):
            pe.wait_ge(squeeze_in, 16 * SQUEEZE_LOADS)
            pe.wait_ge(prep_dve, 1)
            pe.transpose(psum[:, 4, 0:Y_HI_ROWS], s_cw, ident[0:Y_HI_ROWS, 0:Y_HI_ROWS])
            pe.transpose(psum[0:3, 5, 0:Y_HI_ROWS], s_cb3, ident[0:Y_HI_ROWS, 0:Y_HI_ROWS]).then_inc(prep_mm, 1)
            pe.wait_ge(prep_dve, 2)

            def prepare(im):
                pe.wait_ge(weights_in, 16 * WEIGHT_LOADS)
                for b in range(2):
                    cols = slice(P * b, P * b + P)
                    pe.transpose(psum[:, 3, W * b:W * b + W], s_wx[:, cols], ident[0:W, 0:W])
                    pe.matmul(psum[:, 4, b:b + 1], s_wx[:, cols], s_cols[0:W, 1:2], start=True, stop=True)
                    pe.matmul(psum[:, 4, 2 + b:3 + b], s_w1[0:W, cols], s_cols[0:W, 5:6], start=True, stop=True)
                pe.transpose(psum[:, 5, 0:HID], s_wi.rearrange("p d w -> p (d w)"), ident[:, :])
                pe.transpose(psum[:, 6, 0:W], s_fo, ident[0:W, 0:W]).then_inc(prep_mm, 1)

                pe.wait_ge(prep_dve, 4)
                for b in range(2):
                    pe.matmul(psum[:, 6, 128 + 32 * b:160 + 32 * b], s_wxT[:, b, :, :].rearrange("p d w -> p (d w)"),
                              s_bdqk, start=True, stop=True)
                    pe.matmul(psum[0:3, 7, 32 * b:32 * b + 32], s_u3[:, b, :], s_bdqk, start=True, stop=True)
                    pe.matmul(psum[:, 3, W * b:W * b + W], s_bdv, s_wxT[:, b, 0, :], start=True, stop=True)
                    mm = pe.matmul(psum[:, 4, b:b + 1], s_bdv, s_cols[:, 8 + b:9 + b], start=True, stop=True)
                mm.then_inc(prep_mm, 1)

                pe.wait_ge(prep_dve, 5)
                for b in range(2):
                    pe.matmul(psum[0:W, 5 + b, 0:4 * W], s_vxT[:, b, :], s_wom[:, b, :, :], start=True, stop=True)
                for b in range(2):
                    mm = pe.matmul(psum[:, 7, 64:64 + W], s_vbx[:, b, :], s_wo[:, b, :], start=(b == 0), stop=False)
                mm = pe.matmul(psum[:, 7, 64:64 + W], headcols[0:1, 0, :], s_brf[0:1, B_ATT:B_ATT + W], start=False,
                               stop=True)
                mm.then_inc(prep_mm, 1)
                pe.wait_ge(prep_dve, PREP_DVE)

            def experts(im):
                for n in range(8):
                    pe.wait_ge(experts_sum, n // 4 + 1)
                    if n >= 2:
                        pe.wait_ge(freed[6 + n % 2], n // 2)
                    for k in range(4):
                        mm = pe.transpose(psum[:, 6 + n % 2, HID * k:HID * k + HID], e_nat[n // 4][:, 4 * (n % 4) + k, :],
                                          ident[:, :])
                    mm.then_inc(filled[6 + n % 2], 1)
                pe.wait_ge(experts_sum, 3)
                pe.wait_ge(freed[6], EXPERT_TURNS[6] - 1)
                pe.transpose(psum[:, 6, 0:LAYERS * EXPERTS], e_b[:, 0, :], ident[0:32, 0:32]).then_inc(filled[6], 1)

            def bias(b, a, n, reps):
                pe.matmul(psum[:, b, :], ones3[:, 0:P], bias_rows[:, a:a + n].unsqueeze(1).to_broadcast([3, reps, n]),
                          start=True, stop=False, skip_group_check=True)

            def conv(im, c):
                if c == 0:
                    pe.wait_ge(x_in, 32 * im.i + 32)
                b = bank_a.claim(pe, im, "conv", c)
                pe.matmul(psum[0:Y_HI_ROWS, b, :], bias_rows[:, B_CONV:B_CONV + Y_HI_ROWS], ones3[:, :], start=True,
                          stop=False)
                pe.matmul(psum[0:Y_HI_ROWS, b, :], conv_w[:, :], xpad[:, 1 + TPC * c:1 + TPC * c + TPC, 1:W + 1],
                          start=False, stop=True).then_inc(filled[b], 1)

            def filters(im, hh, r):
                if isinstance(im.i, int) and im.i == 0 and (hh, r) == (0, 0):
                    pe.wait_ge(prep_dve, 3)
                b = bank_a.claim(pe, im, "filters", hh, r,
                                 needs=[("conv", c) for c in range(CHUNKS)] if (hh, r) == (0, 0) else [])
                y = y16[:, :].rearrange("p (g r a w) -> p g r a w", r=PR, a=WP, w=PW)[:, :, r, :, :]
                o = psum[0:PK, b, :].rearrange("p (g a w) -> p g a w", a=WP, w=PW)
                for k in range(3):
                    mm = pe.matmul(o[:, :, :, k::3], tap_w[:, hh, r, k, :, :].rearrange("p i j -> p (i j)"),
                                   y[:, :, :, k::3], start=True, stop=True)
                mm.then_inc(filled[b], 1)

            def patches(im, g):
                b = bank_a.claim(pe, im, "patches", g)
                pe.wait_ge(regrouped, RG * im.i + (g + 1))
                for a in range(WP):
                    mm = pe.transpose(psum[0:PK, b, P * a:P * a + P],
                                      xrun[:, g % 4, a, :, :].rearrange("p i j -> p (i j)"), ident[:, :])
                mm.then_inc(filled[b], 1)

            def involve(im, c):
                needs = [("patches", 2 * c)]
                if c == 0:
                    needs += [("filters", hh, r) for hh in range(2) for r in range(PR)]
                b = bank_a.claim(pe, im, "involve", c, needs=needs)
                for g in (2 * c, 2 * c + 1):
                    if g % 2:
                        bank_a.taken(pe, im, "patches", g)
                    for a in range(WP):
                        for hh in range(2):
                            rows = slice(CH * hh, CH * hh + CH)
                            o = psum[rows, b, 256 * (g % 2):256 * (g % 2) + 256].rearrange("p (r w) -> p r w", w=W)
                            f = filt[hh].rearrange("p (t w) -> p t w", w=W)
                            mm = pe.matmul(o[:, :, PW * a:PW * a + PW], xpatch[:, g % 4, a, rows],
                                           f[:, PR * g:PR * g + PR, PW * a:PW * a + PW], start=True, stop=True)
                mm.then_inc(filled[b], 1)

            def zt(im, c):
                if c % 2 == 0:
                    pe.wait_ge(zn_ready, 2 * im.i + (c // 2 + 1))
                b = bank_b.claim(pe, im, "zt", c)
                for k in range(4):
                    n = CW * c + P * k
                    mm = pe.transpose(psum[:, b, P * k:P * k + P], zn[:, n:n + P], ident[:, :])
                mm.then_inc(filled[b], 1)

            def logits(im, c):
                b = bank_b.claim(pe, im, "logits", c, needs=[("zt", c)])
                bias(b, B_QK, 2 * HKR, TPC)
                for k in range(4):
                    mm = pe.matmul(psum[:, b, P * k:P * k + P], zT[:, c % 2, P * k:P * k + P], qk_w[:, :],
                                   start=False, stop=True, skip_group_check=True)
                mm.then_inc(filled[b], 1)

            def kmax(im):
                b = bank_b.claim(pe, im, "kmax")
                pe.wait_ge(k_step, K_STEPS * im.i + 1)
                pe.transpose(psum[0:HKR, b, 0:P], kmx[:, :], ident[:, :]).then_inc(filled[b], 1)

            def kshift(im):
                b = bank_b.claim(pe, im, "kshift", needs=[("kmax",)])
                pe.matmul(psum[:, b, 0:HKR], kmb[:, :], ident[0:HKR, 0:HKR], start=True, stop=True).then_inc(filled[b], 1)

            def pool(im):
                b = bank_b.claim(pe, im, "pool")
                pe.wait_ge(k_exp, im.i + 1)
                for t in range(HR):
                    pe.matmul(psum[0:W, b, 0:HKR], zn[:, W * t:W * t + W], lg[:, t, HKR:2 * HKR], start=(t == 0),
                              stop=(t == HR - 1))
                pe.wait_ge(k_step, K_STEPS * im.i + 4)
                pe.matmul(psum[:, b, 64:65], ksum[:, :, :].rearrange("p a k -> p (a k)"), ones_col[:, :], start=True,
                          stop=True).then_inc(filled[b], 1)

            def mix(im):
                b = bank_b.claim(pe, im, "mix", needs=[("pool",)])
                for h in range(HEADS):
                    mm = pe.matmul(psum[0:W, b, KR * h:KR * h + KR], head_w[:, h, :], khT[:, KR * h:KR * h + KR],
                                   start=True, stop=True)
                mm.then_inc(filled[b], 1)

            def mixt(im):
                b = bank_b.claim(pe, im, "mixt", needs=[("mix",)])
                pe.transpose(psum[:, b, 0:P], gT4[:, :, :].rearrange("p a k -> p (a k)"), ident[:, :]
                             ).then_inc(filled[b], 1)

            def qt(im, j):
                if j == 0:
                    pe.wait_ge(q_step, Q_STEPS * im.i + Q_STEPS)
                b = bank_b.claim(pe, im, "qt", j)
                for k in range(4):
                    t = 16 * j + 4 * k
                    mm = pe.transpose(psum[:, b, P * k:P * k + P], q[:, t:t + 4, :].rearrange("p t k -> p (t k)"),
                                      ident[:, :])
                mm.then_inc(filled[b], 1)

            def attend(im, c):
                b = bank_b.claim(pe, im, "attend", c, needs=[("qt", c // 2)])
                if c == 0:
                    bank_b.taken(pe, im, "mixt")
                for k in range(2):
                    mm = pe.matmul(psum[:, b, 256 * k:256 * k + 256], qT[:, 2 * c + k, :],
                                   gmix[:, :, :].rearrange("p k w -> p (k w)"), start=True, stop=True)
                mm.then_inc(filled[b], 1)

            def turn16(b, src, c):
                o = psum[:, b, :].bitcast(F16)
                for k in range(TPC):
                    mm = pe.transpose(o[:, P * k:P * k + P], src[:, TPC * c + k, :], ident16[:, :])
                mm.then_inc(filled[b], 1)

            def ft(im, c):
                if c % 2 == 0:
                    pe.wait_ge(lo2, 2 * im.i + (c // 2 + 1))
                turn16(bank_m.claim(pe, im, "ft", c), sp2, c)

            def z3t(im, c):
                if c % 2 == 0:
                    pe.wait_ge(lo3, 2 * im.i + (c // 2 + 1))
                turn16(bank_c.claim(pe, im, "z3t", c), sp3, c)

            def w1(im, c, k):
                b = bank_m.claim(pe, im, "w1", c, k, needs=[("ft", c)])
                f, x = slice(P * (k % 2), P * (k % 2) + P), fT[:, c % 2, 512 * (k // 2):512 * (k // 2) + 512]
                pe.matmul(psum[:, b, :], w1_hh[:, f], x, start=True, stop=False)
                pe.matmul(psum[:, b, :], w1_l0[:, f], x, start=False, stop=True).then_inc(filled[b], 1)

            def w2(im, c, k):
                if k == 0:
                    bias(bank_w2.claim(pe, im, "w2", c), B_MLP, W, TPC)
                b = bank_w2.place["w2", c][0]
                u = 2 * c + k // 2
                if k % 2 == 0:
                    pe.wait_ge(ge_low, 2 * CHUNKS * im.i + (u + 1))
                for t in (2 * k, 2 * k + 1):
                    n = P * (t % 4)
                    for f in range(2):
                        for g, w in ((ge_hi, w2_hi), (ge_hi, w2_lo), (ge_lo, w2_hi)):
                            mm = pe.matmul(psum[:, b, W * t:W * t + W], g[:, u % 3, f, n:n + P], w[:, f, :],
                                           start=False, stop=(f == 1 and g is ge_lo), skip_group_check=True)
                if k == 3:
                    mm.then_inc(filled[b], 1)

            def ffn(im, t):
                if t < SEGS:
                    b = bank_c.claim(pe, im, "wi", t, needs=[("z3t", c) for c in range(CHUNKS)])
                    x = z3T[:, :, :, SEGC * t:SEGC * t + SEGC]
                    pe.matmul(psum[:, b, :], wi_hh[:, :], x, start=True, stop=False)
                    pe.matmul(psum[:, b, :], wi_l0[:, :], x, start=False, stop=True).then_inc(filled[b], 1)
                if 1 <= t <= SEGS:
                    s = t - 1
                    b = bank_c.claim(pe, im, "e1", s, needs=[("wi", s)])
                    pe.wait_ge(ew_in[s % WE_RING], 16 * (SEGS // WE_RING) * im.i + 16 * (s // WE_RING + 1))
                    pe.matmul(psum[:, b, :], ew[:, s % WE_RING, 0:HID], hid_a[:, s % 2, :], start=True,
                              stop=True).then_inc(filled[b], 1)
                if t >= 2:
                    s = t - 2
                    b = bank_c.claim(pe, im, "e2", s, needs=[("e1", s)])
                    pe.matmul(psum[:, b, :], ew[:, s % WE_RING, HID:2 * HID], hid_b[:, s % 2, :], start=True,
                              stop=True).then_inc(filled[b], 1)

            def ffn_out(im, c):
                if c == 0:
                    pe.wait_ge(hid_low, SEGS * im.i + SEGS)
                b = bank_c.claim(pe, im, "out", c)
                bias(b, B_FFN, W, TPC)
                for k in range(TPC):
                    for h, w in ((hid_hi, fo_hi), (hid_hi, fo_lo), (hid_lo, fo_hi)):
                        mm = pe.matmul(psum[:, b, W * k:W * k + W],
                                       h[:, TPC * c + k, :, :].rearrange("p hh c -> p (hh c)"), w[:, :], start=False,
                                       stop=(h is hid_lo), skip_group_check=True)
                mm.then_inc(filled[b], 1)

            slots(pe, {"conv": conv, "filters": filters, "patches": patches, "involve": involve, "zt": zt,
                       "logits": logits, "kmax": kmax, "kshift": kshift, "pool": pool, "mix": mix, "mixt": mixt,
                       "qt": qt, "attend": attend, "ft": ft, "z3t": z3t, "w1": w1, "w2": w2, "ffn": ffn,
                       "out": ffn_out}, first={"prepare": prepare}, second={"experts": experts})


_INS = ["x", "L0_tok_conv1_w", "L0_tok_conv1_b", "L0_tok_bn_gamma", "L0_tok_bn_beta", "L0_tok_bn_mean",
        "L0_tok_bn_var", "L0_tok_conv2_w", "L0_tok_conv2_b", "L0_attn_ln1_g", "L0_attn_ln1_b", "L0_attn_Wx",
        "L0_attn_bx", "L0_attn_Wq", "L0_attn_Wk", "L0_attn_Wv", "L0_attn_Wo", "L0_attn_bo", "L0_attn_ln2_g",
        "L0_attn_ln2_b", "L0_attn_W1", "L0_attn_b1", "L0_attn_W2", "L0_attn_b2", "L0_ffn_route_id", "L0_ffn_Wi",
        "L0_ffn_bi", "L0_ffn_Wr", "L0_ffn_br", "L0_ffn_Ws", "L0_ffn_bs", "L0_ffn_Wo", "L0_ffn_bo"]


def constants():
    eye = np.eye(P, dtype=np.float32)
    band = np.zeros((PR + 2, PW + 2, WP, PW), np.float32)
    for w in range(PW):
        band[:, w:w + 3, :, w] = 1
    head = np.arange(P) // DH
    cols = np.tile(np.repeat(np.arange(HEADS), KR), 4)
    headcols = np.stack([(4 * b + head)[:, None] == cols[None, :] for b in range(2)], 1).astype(np.float32)
    headrows = (head[:, None] == np.arange(4)[None, :]).astype(np.float32)
    ypick = np.zeros((Y_ROWS, 2, 3), np.float32)
    for g, (hh, part) in enumerate(((0, 0), (0, 1), (1, 0), (1, 1), (0, 0), (1, 0))):
        ypick[CR * g:CR * g + CR, hh, part] = 1
    for part in range(3):
        ypick[Y_ONE_ROW + part, :, part] = 1
    halfpick = (np.repeat(GROUP_HALF, CR)[:, None] == np.arange(2)[None, :]).astype(np.float32)
    parts = {"ident": eye, "bandmask": band.reshape(PK, W), "headcols": headcols.reshape(P, 2 * P),
             "headrows": headrows, "ypick": ypick.reshape(Y_ROWS, 6), "halfpick": halfpick}
    return {"constants": np.concatenate([np.pad(parts[n], ((0, P - len(parts[n])), (0, 0))) for n, w in CONSTANTS], 1)}


def kernel(**inputs):
    import concourse.bacc as _bacc
    from concourse.bass_utils import run_bass_kernel_spmd as _run

    nc = _bacc.Bacc("TRN2", target_bir_lowering=False, num_devices=1)
    arrays, args = {}, {}
    for name, a in [(n, inputs[n]) for n in _INS] + list(constants().items()):
        a = np.ascontiguousarray(a)
        arrays[f"in_{name}"] = a
        args[name] = nc.dram_tensor(f"in_{name}", a.shape, mybir.dt.from_np(a.dtype), kind="ExternalInput").ap()
    out = nc.dram_tensor("out_0", (IMAGES, CH * ROWS, W), F32, kind="ExternalOutput").ap()
    tower_kernel(nc, args, out)
    r = _run(nc, [arrays], core_ids=[0])
    return r.results[0]["out_0"]
```
